# Optimizing a Trainium2 kernel written in Bass

```python
import numpy as np
import jax
import jax.numpy as jnp

def _softmax(x, axis=-1):
    return jax.nn.softmax(x, axis=axis)

def _gelu(x):
    return jax.nn.gelu(x, approximate=True)

def _silu(x):
    return jax.nn.silu(x)

def _sigmoid(x):
    return jax.nn.sigmoid(x)

def _layernorm(x, axis=-1, eps=1e-05):
    m = jnp.mean(x, axis=axis, keepdims=True)
    v = jnp.var(x, axis=axis, keepdims=True)
    return (x - m) / jnp.sqrt(v + eps)

def _scatter_add(tgt, idx, src, axis=0):
    return tgt.at[idx].add(src)

def _segment_sum(src, seg, n):
    return jax.ops.segment_sum(src, seg, n)
kernel_name = 'mk_xattn_ffn_d1_seqx_r8_7a9b1c'

def setup_inputs(seed: int=0):
    np.random.seed(seed)
    _w = jnp.asarray

    def _rec_inputs():
        import jax
        import jax.numpy as jnp
        _rk = jax.random.key(seed)
        x = -0.0002928 + 1 * jax.random.normal(jax.random.fold_in(_rk, 1), (8, 56, 128), jnp.float32)
        _lenS = 56 - jax.random.randint(jax.random.fold_in(_rk, 7), (8,), 0, max(1, 56 // 4) + 1, jnp.int32)
        _lenS2 = 1500 - jax.random.randint(jax.random.fold_in(_rk, 8), (8,), 0, max(1, 1500 // 4) + 1, jnp.int32)
        _ctx_768P = jax.random.normal(jax.random.fold_in(_rk, 11), (8, 16, 96), jnp.float32)
        _ctx_768c = jax.random.dirichlet(jax.random.fold_in(_rk, 511), 0.3 * jnp.ones((16,), jnp.float32), (8, 1500))
        _ctx_768t = jnp.einsum('bsk,bkd->bsd', _ctx_768c, _ctx_768P)
        _ctx_768t = _ctx_768t * jax.lax.rsqrt(jnp.mean(jnp.square(_ctx_768t)) + 1e-12) * 0.953939
        ctx_768 = 2.09791e-05 + 1.00001 * (_ctx_768t + 0.3 * jax.random.normal(jax.random.fold_in(_rk, 611), (8, 1500, 96), jnp.float32))
        return (x, ctx_768)
    x, ctx_768 = _rec_inputs()

    def _L0_xattn_setup():
        import jax, jax.numpy as jnp
        import numpy as np
        N_HEADS = 16
        D_HEAD = 64
        key = jax.random.key(seed)
        ks = jax.random.split(key, 7)
        B, SQ, SKV = (2, 256, 256)
        D_MODEL, D_COND, D_ATTN = (128, 96, N_HEADS * D_HEAD)
        return {'x': jax.random.normal(ks[0], (B, SQ, D_MODEL), jnp.float32), 'cond': jax.random.normal(ks[1], (B, SKV, D_COND), jnp.float32), 'w_q': jax.random.normal(ks[2], (D_MODEL, D_ATTN), jnp.float32) * D_MODEL ** (-0.5), 'w_k': jax.random.normal(ks[3], (D_COND, D_ATTN), jnp.float32) * D_COND ** (-0.5), 'w_v': jax.random.normal(ks[4], (D_COND, D_ATTN), jnp.float32) * D_COND ** (-0.5), 'w_out': jax.random.normal(ks[5], (D_ATTN, D_MODEL), jnp.float32) * D_ATTN ** (-0.5), 'b_out': jnp.zeros((D_MODEL,), jnp.float32)}
    _L0_xattn_all = _L0_xattn_setup()
    _L0_xattn_in = {k: v for k, v in _L0_xattn_all.items() if k in ('w_q', 'w_k', 'w_v', 'w_out', 'b_out')}
    del _L0_xattn_all

    def _L0_ffn_setup():
        import jax, jax.numpy as jnp
        import numpy as np
        INT8_MAX = 127.0

        def _absmax_scale(x, axes):
            amax = jnp.max(jnp.abs(x), axis=axes, keepdims=True)
            return jnp.maximum(amax, 1e-12) / INT8_MAX
        key = jax.random.key(seed)
        k1, k2 = jax.random.split(key)
        lhs = jax.random.normal(k1, (4, 1024, 128), dtype=jnp.float32)
        rhs = jax.random.normal(k2, (128, 128), dtype=jnp.float32)
        return {'lhs': lhs, 'rhs': rhs}
    _L0_ffn_all = _L0_ffn_setup()
    _L0_ffn_in = {k: v for k, v in _L0_ffn_all.items() if k in ('rhs',)}
    del _L0_ffn_all
    return {'x': x, 'ctx_768': ctx_768, 'L0_xattn_w_q': _L0_xattn_in['w_q'], 'L0_xattn_w_k': _L0_xattn_in['w_k'], 'L0_xattn_w_v': _L0_xattn_in['w_v'], 'L0_xattn_w_out': _L0_xattn_in['w_out'], 'L0_xattn_b_out': _L0_xattn_in['b_out'], 'L0_ffn_rhs': _L0_ffn_in['rhs']}

def reference(x, ctx_768, L0_xattn_w_q, L0_xattn_w_k, L0_xattn_w_v, L0_xattn_w_out, L0_xattn_b_out, L0_ffn_rhs):
    import jax
    import jax.numpy as jnp

    def _L0_xattn_ref(x, cond, w_q, w_k, w_v, w_out, b_out):
        import jax, jax.numpy as jnp
        import numpy as np
        N_HEADS = 16
        D_HEAD = 64
        B, SQ, _ = x.shape
        SKV = cond.shape[1]
        scale = D_HEAD ** (-0.5)
        q = (x @ w_q).reshape(B, SQ, N_HEADS, D_HEAD)
        k = (cond @ w_k).reshape(B, SKV, N_HEADS, D_HEAD)
        v = (cond @ w_v).reshape(B, SKV, N_HEADS, D_HEAD)
        attn = jnp.einsum('bqhd,bkhd->bhqk', q, k) * scale
        attn = jax.nn.softmax(attn, axis=-1)
        out = jnp.einsum('bhqk,bkhd->bqhd', attn, v).reshape(B, SQ, N_HEADS * D_HEAD)
        return out @ w_out + b_out

    def _L0_ffn_ref(lhs, rhs):
        import jax, jax.numpy as jnp
        import numpy as np
        INT8_MAX = 127.0

        def _absmax_scale(x, axes):
            amax = jnp.max(jnp.abs(x), axis=axes, keepdims=True)
            return jnp.maximum(amax, 1e-12) / INT8_MAX
        lhs_scale = _absmax_scale(lhs, (2,))
        rhs_scale = _absmax_scale(rhs, (0,))
        q_lhs = jnp.clip(jnp.round(lhs / lhs_scale), -INT8_MAX, INT8_MAX).astype(jnp.int8)
        q_rhs = jnp.clip(jnp.round(rhs / rhs_scale), -INT8_MAX, INT8_MAX).astype(jnp.int8)
        acc = jax.lax.dot_general(q_lhs, q_rhs, (((2,), (0,)), ((), ())), preferred_element_type=jnp.int32)
        return acc.astype(jnp.float32) * lhs_scale * rhs_scale
    x = x + _L0_xattn_ref(_layernorm(x, axis=-1), ctx_768, L0_xattn_w_q, L0_xattn_w_k, L0_xattn_w_v, L0_xattn_w_out, L0_xattn_b_out)
    x = x + _L0_ffn_ref(_layernorm(x, axis=-1), L0_ffn_rhs)
    return x

_drawn_inputs = setup_inputs


def setup_inputs(seed=0):
    import zlib

    import numpy as np

    out = dict(_drawn_inputs(seed))
    spreads = {'L0_xattn_b_out': (0.0, 0.1)}
    factors = {}
    for name, (base, spread) in spreads.items():
        noise = np.random.default_rng([zlib.crc32(name.encode()), seed]).standard_normal(out[name].shape)
        drawn = base * np.exp(spread * noise) if base else spread * noise
        out[name] = jnp.asarray(drawn.astype(out[name].dtype))
    for name, factor in factors.items():
        out[name] = (out[name] * factor).astype(out[name].dtype)
    return out
```

```python
from contextlib import ExitStack

import concourse.bass as bass
from concourse import mybir

F32 = mybir.dt.float32
F16 = mybir.dt.float16
BF16 = mybir.dt.bfloat16
ALU = mybir.AluOpType
ACT = mybir.ActivationFunctionType
AX = mybir.AxisListType

B, Q, D = 8, 56, 128
KV, DC = 1500, 96
H, DH = 16, 64
KP = 125
NT = KV // KP
ROWS = H * Q
HALF = ROWS // 2
NR = ROWS // 128
NC = 3
TC = NT // NC
CW = KV // NC
CN = 2 * DC + 1
PAIR = 2 * Q
NP = B // 2
HG = H // 2
LAG = 2
NPB = 4
SCALE = DH ** -0.5
EPS = 1e-5
QMAX = 127.0
ROUND = 1.5 * 2.0 ** 23
LN_XN = 2 * NP + 1
NFFN = 10

LO_DVE = [(j, 0) for j in range(NT) if j % 3 != 1]
LO_POOL = [(j, h) for j in range(NT) for h in (1, 0) if (j, h) not in LO_DVE]

PREP_HEAD = [(0, 0, "ct", 0), (0, 1, "ct", 1), (1, 0, "ct", 2), (1, 1, "g", 0), (2, 0, "g", 1)]
UT = [(4, 0, "ut", 0), (4, 1, "ut", 1)]
RHS = [(4, 0, "rhs", 0), (6, 0, "rhs", 1)]
OUT = [(5, 0, "out", 0), (8, 0, "ft", 0), (9, 0, "fm", 0)]
MAX_AT = [(3, 0), (3, 1), (3, 2), (4, 2), (5, 1), (5, 2), (6, 0), (6, 1), (6, 2), (7, 0), (7, 1),
          (7, 2), (8, 0), (8, 1), (8, 2), (9, 0), (9, 1), (9, 2), (10, 0), (10, 1), (10, 2)]
MAXES = [(j, a, "max", m) for m, (j, a) in enumerate(MAX_AT)]
MROW = [(11, 1, "mrow", 0), (11, 2, "mrow", 1)]


def in_order(*lists):
    return [(what, m, j, a) for j, a, _, what, m in
            sorted((j, a, n, what, m) for n, l in enumerate(lists) for j, a, what, m in l)]


PREP = [(what, m, 0, 0) for l in (PREP_HEAD, MAXES, MROW) for _, _, what, m in l]
FIRST = in_order(RHS, PREP_HEAD, MAXES, MROW)
ODD = in_order(UT, PREP_HEAD, MAXES, MROW)
EVEN = in_order(OUT, UT, PREP_HEAD, MAXES, MROW)
LAST = in_order(UT)
TAIL = [("ut", 0, 0, 0), ("ut", 1, 0, 0), ("out", 0, 0, 0), ("ft", 0, 0, 0), ("fm", 0, 0, 0)]


def uses(schedule, bank):
    return (len(schedule) + 1 - bank) // 2


class Step:

    def __init__(self, t0, schedule, i=None):
        self.t0, self.i, self.schedule = t0, i, schedule
        self.odd = t0 % 2

    def times(self, per, more=0):
        fixed = per * self.t0 + more
        return fixed if self.i is None else self.i * (2 * per) + fixed

    def pairs(self, per, more=0):
        fixed = per * ((self.t0 - 1) // 2) + more
        return fixed if self.i is None else self.i * per + fixed

    def freed(self, k):
        bank = k % 2
        fixed = uses(PREP, bank) + k // 2
        if self.t0 > 0:
            fixed += uses(FIRST, bank)
        if self.i is not None:
            if not self.odd:
                fixed += uses(ODD, bank)
            return self.i * (uses(ODD, bank) + uses(EVEN, bank)) + fixed
        if self.t0 > 0:
            fixed += 3 * (uses(ODD, bank) + uses(EVEN, bank))
        if self.t0 > B - 1:
            fixed += uses(LAST, bank)
        return fixed


class Prologue(Step):

    def __init__(self):
        super().__init__(-1, PREP)
        self.odd = 1

    def freed(self, k):
        return k // 2


def at_least(eng, sem, value):
    if not isinstance(value, int) or value > 0:
        eng.wait_ge(sem, value)


def run_steps(eng, step):
    step(Step(0, FIRST))
    with eng.Fori(0, (B - 2) // 2) as i:
        step(Step(1, ODD, i))
        step(Step(2, EVEN, i))
    step(Step(B - 1, LAST))


def at(schedule, j, place):
    return [(k, what, m) for k, (what, m, jj, a) in enumerate(schedule) if (jj, a) == (j, place)]


def build(nc, x, ctx_kv, w_q, w_k, w_v, w_out, b_out, rhs, out):
    with ExitStack() as stack:
        def sb(name, shape, dt):
            return stack.enter_context(nc.sbuf_tensor(name, shape, dt))

        def psum(name, shape, dt):
            return stack.enter_context(nc.psum_tensor(name, shape, dt))

        def sem(name):
            return stack.enter_context(nc.semaphore(name))

        scores = psum("scores", [128, 2, 512], F32)
        side = psum("side", [128, 2, 512], F32)
        pc = psum("pc", [128, 4, 512], F32)

        ident = sb("ident", [128, 128], F32)
        ident16 = sb("ident16", [128, 128], F16)
        ones = sb("ones", [128, PAIR], F32)
        minus_half = sb("minus_half", [128, NP], F32)
        wq = sb("wq", [D, H * DH], F32)
        wk = sb("wk", [DC, H * DH], F32)
        wv = sb("wv", [DC, H * DH], F32)
        wo = sb("wo", [128, H // 2, D], F32)
        wqT = sb("wqT", [128, H // 2, D], F32)
        wkT = sb("wkT", [128, H // 2, DC], F32)
        wvT = sb("wvT", [128, H // 2, DC], F32)
        G = sb("G", [D, H, DC], F32)
        M = sb("M", [DC, H, D], F32)
        bias = sb("bias", [PAIR, D], F32)
        rhs_in = sb("rhs_in", [D, D], F32)
        rhsT_q = sb("rhsT_q", [D, D], F32)
        rhsT_i = sb("rhsT_i", [D, D], F16)
        rhs_i = sb("rhs_i", [D, D], F16)
        rhs_sc = sb("rhs_sc", [D, 4], F32)
        rhs_diag = sb("rhs_diag", [D, D], F32)
        rhs_row = sb("rhs_row", [PAIR, D], F32)

        x_in = sb("x_in", [PAIR, NP, D], F32)
        xn = sb("xn", [PAIR, NP, D], F32)
        xb = sb("xb", [PAIR, NP, D], F32)
        xnT = sb("xnT", [D, B * Q], F32)
        st1 = sb("st1", [PAIR, NP, 6], F32)
        mv1 = sb("mv1", [PAIR, NP, 2], F32)
        ve1 = sb("ve1", [PAIR, NP], F32)
        rstd1 = sb("rstd1", [PAIR, NP], F32)

        c32 = sb("c32", [KP, 2, NT, DC], F32)
        cn = sb("cn", [KP, 2, NT, CN + 1], F16)
        cT_hi = sb("cT_hi", [DC + 1, 2, KV], F16)
        cT_lo = sb("cT_lo", [DC, 2, KV], F16)
        g_hi = sb("g_hi", [DC, 2, ROWS], F16)
        g_lo = sb("g_lo", [DC + 1, 2, ROWS], F16)
        maxes = sb("maxes", [128, NR, NC], F32)
        neg_max = sb("neg_max", [128, NR], F16)
        prob = sb("prob", [KP, NPB, ROWS], F32)
        prob_lo = sb("prob_lo", [KP, NPB, ROWS], F16)
        rsum = sb("rsum", [128, NR], F32)
        u_part = sb("u_part", [128, NR, CN], F32)
        u = sb("u", [128, NR, DC], F32)
        uT = sb("uT", [DC, H, 2, Q], F32)

        x1 = sb("x1", [PAIR, D], F32)
        st2 = sb("st2", [PAIR, 6], F32)
        mv2 = sb("mv2", [PAIR, 2], F32)
        ve2 = sb("ve2", [PAIR, 1], F32)
        rstd2 = sb("rstd2", [PAIR, 1], F32)
        xn2 = sb("xn2", [PAIR, D], F32)
        row_sc = sb("row_sc", [PAIR, 3], F32)
        q_a = sb("q_a", [PAIR, D], F32)
        q_b = sb("q_b", [PAIR, D], F32)
        q_i = sb("q_i", [PAIR, D], F16)
        q_iT = sb("q_iT", [D, PAIR], F16)
        y_a = sb("y_a", [PAIR, D], F32)
        y = sb("y", [PAIR, NP, D], F32)

        prob_hi = prob[:, :, :].bitcast(BF16).rearrange("p b (n two) -> p b n two", two=2)[:, :, :, 1]

        x_loaded, wq_loaded, wk_loaded = sem("x_loaded"), sem("wq_loaded"), sem("wk_loaded")
        wv_loaded, wo_loaded, rhs_loaded = sem("wv_loaded"), sem("wo_loaded"), sem("rhs_loaded")
        bias_loaded = sem("bias_loaded")
        c_loaded = [sem("c_loaded_even"), sem("c_loaded_odd")]
        out_stored = sem("out_stored")
        const_ready = sem("const_ready")
        w_full, w_taken = sem("w_full"), sem("w_taken")
        wk_taken = sem("wk_taken")
        ln_step, ln_rstd = sem("ln_step"), sem("ln_rstd")
        xnT_full, xnT_ready = sem("xnT_full"), sem("xnT_ready")
        rhs_step = sem("rhs_step")
        const_step, late_const = sem("const_step"), sem("late_const")
        minus_half_ready, g_ready, xb_ready = sem("minus_half_ready"), sem("g_ready"), sem("xb_ready")
        scores_full = sem("scores_full")
        pc_done = sem("pc_done")
        ct_full, g_full = sem("ct_full"), sem("g_full")
        max_full, mrow_full = sem("max_full"), sem("mrow_full")
        ut_full = sem("ut_full")
        out_full, ft_full, fm_full = sem("out_full"), sem("ft_full"), sem("fm_full")
        rhs_full = sem("rhs_full")
        side_free = [sem("side0_free"), sem("side1_free")]
        exp_done = sem("exp_done")
        ct_hi_done, g_hi_done = sem("ct_hi_done"), sem("g_hi_done")
        c_hi_done = sem("c_hi_done")
        lo_pool = sem("lo_pool")
        c_lo_done = sem("c_lo_done")
        u_done = sem("u_done")
        rstd2_done = sem("rstd2_done")
        lo_dve = sem("lo_dve")
        neg_max_done = sem("neg_max_done")
        rsum_done, u_part_done = sem("rsum_done"), sem("u_part_done")
        ffn_step = sem("ffn_step")
        y_done = sem("y_done")

        block = stack.enter_context(nc.Block())

        c_dram = ctx_kv.rearrange("b (p j) d -> b p j d", j=NT)
        x_dram = x.rearrange("(n two) q d -> (two q) n d", two=2)
        out_dram = out.rearrange("(n two) q d -> n (two q) d", two=2)

        @block.sync
        def _(sp):
            sp.dma_start(x_in[:, :, :], x_dram).then_inc(x_loaded, 16)
            sp.dma_start(c32[:, 0], c_dram[0]).then_inc(c_loaded[0], 16)
            sp.dma_start(wk[:, :], w_k).then_inc(wk_loaded, 16)
            sp.dma_start(wv[:, :], w_v).then_inc(wv_loaded, 16)
            sp.dma_start(wo[:, :, :], w_out.rearrange("(b p) n -> p b n", p=128)).then_inc(wo_loaded, 16)
            sp.dma_start(c32[:, 1], c_dram[1]).then_inc(c_loaded[1], 16)
            sp.dma_start(rhs_in[:, :], rhs).then_inc(rhs_loaded, 16)
            for b in range(2, B):
                sp.wait_ge(ct_full, NC * (b - 1))
                sp.wait_ge(c_lo_done, b - 1)
                sp.dma_start(c32[:, b % 2], c_dram[b]).then_inc(c_loaded[b % 2], 16)
                if b >= 5 and b % 2 == 1:
                    p = (b - 5) // 2
                    sp.wait_ge(y_done, p + 1)
                    sp.dma_start(out_dram[p], y[:, p, :]).then_inc(out_stored, 16)
            for p in range(2, NP):
                sp.wait_ge(y_done, p + 1)
                sp.dma_start(out_dram[p], y[:, p, :]).then_inc(out_stored, 16)
            sp.wait_ge(out_stored, 16 * NP)

        @block.tensor
        def _(pe):
            def side_bank(s, k):
                at_least(pe, side_free[k % 2], s.freed(k))
                return side[:, k % 2]

            def transpose_c(s, k, c):
                n2 = (s.t0 + 1) % 2
                if c == 0:
                    at_least(pe, c_loaded[n2], s.times(8, 24 if not n2 else 16))
                bank = side_bank(s, k)
                for jj in range(TC):
                    mm = pe.transpose(bank[0:DC, jj * KP:(jj + 1) * KP], c32[:, n2, c * TC + jj],
                                      ident[0:KP, 0:KP])
                mm.then_inc(ct_full, 1)

            def make_g(s, k, half):
                bank = side_bank(s, k)
                if s.i is None:
                    xt = xnT[:, s.times(Q, Q):s.times(Q, Q) + Q]
                else:
                    xt = xnT[:, bass.ds(s.times(Q, Q), Q)]
                for h in range(HG):
                    mm = pe.matmul(bank[0:DC, h * Q:(h + 1) * Q], G[:, half * HG + h, :], xt,
                                   start=True, stop=True)
                mm.then_inc(g_full, 1)

            def first_pass(s, k, m):
                n2 = (s.t0 + 1) % 2
                r, c = m // NC, m % NC
                if m == 0:
                    pe.wait_ge(ct_hi_done, s.times(NC, 2 * NC))
                    pe.wait_ge(g_hi_done, s.times(2, 4))
                bank = side_bank(s, k)
                pe.matmul(bank[:, 0:CW], g_hi[:, n2, r * 128:(r + 1) * 128],
                          cT_hi[0:DC, n2, c * CW:(c + 1) * CW], start=True, stop=True).then_inc(max_full, 1)

            def turn_max(s, k, m):
                bank = side_bank(s, k)
                if m == 0:
                    pe.wait_ge(neg_max_done, s.times(1, 2))
                for r in range(4 * m, min(4 * m + 4, NR)):
                    mm = pe.matmul(bank[DC:DC + 1, (r % 4) * 128:(r % 4 + 1) * 128], neg_max[:, r:r + 1],
                                   ident16[:, :], start=True, stop=True)
                mm.then_inc(mrow_full, 1)

            def turn_u(s, k, m):
                bank = side_bank(s, k)
                if m == 0:
                    pe.wait_ge(u_done, s.times(1))
                for r in range(4 * m, min(4 * m + 4, NR)):
                    mm = pe.transpose(bank[0:DC, (r % 4) * 128:(r % 4 + 1) * 128], u[:, r, :], ident[:, :])
                mm.then_inc(ut_full, 1)

            def project_out(s, k, m):
                bank = side_bank(s, k)
                pe.wait_ge(side_free[(k + 1) % 2], s.freed(k + 1))
                for h in range(H):
                    mm = pe.matmul(bank[0:PAIR, 0:D], uT[:, h].rearrange("c b q -> c (b q)"), M[:, h, :],
                                   start=(h == 0), stop=(h == H - 1))
                mm.then_inc(out_full, 1)

            def turn_q(s, k, m):
                bank = side_bank(s, k)
                pe.wait_ge(ffn_step, s.pairs(NFFN, NFFN))
                pe.transpose(bank[:, 0:PAIR // 2].bitcast(F16), q_i[:, :],
                             ident16[0:PAIR, 0:PAIR]).then_inc(ft_full, 1)

            def linear(s, k, m):
                bank = side_bank(s, k)
                kt = [kk for kk, use in enumerate(s.schedule) if use[0] == "ft"][0]
                pe.wait_ge(side_free[kt % 2], s.freed(kt + 2))
                pe.matmul(bank[0:PAIR, 0:D], q_iT[:, :], rhs_i[:, :], start=True, stop=True)\
                    .then_inc(fm_full, 1)

            def rhs_work(s, k, m):
                bank = side_bank(s, k)
                if m == 0:
                    pe.wait_ge(rhs_loaded, 16)
                    pe.transpose(bank[:, 0:D], rhs_in[:, :], ident[:, :]).then_inc(rhs_full, 1)
                else:
                    pe.wait_ge(rhs_step, 6)
                    pe.transpose(bank[:, 0:D // 2].bitcast(F16), rhsT_i[:, :], ident16[:, :])
                    pe.matmul(bank[0:PAIR, D:2 * D], ones[:, :], rhs_diag[:, :], start=True, stop=True)\
                        .then_inc(rhs_full, 1)

            WORK = {"ct": transpose_c, "g": make_g, "max": first_pass, "mrow": turn_max, "ut": turn_u,
                    "out": project_out, "ft": turn_q, "fm": linear, "rhs": rhs_work}

            def side_work(s, j, place):
                for k, what, m in at(s.schedule, j, place):
                    WORK[what](s, k, m)

            def second_pass(s, j, half):
                b2 = s.t0 % 2
                kv = slice(j * KP, (j + 1) * KP)
                cols = slice(half * HALF, (half + 1) * HALF)
                if j == 0 and half == 0:
                    pe.wait_ge(side_free[0], s.freed(0))
                    pe.wait_ge(side_free[1], s.freed(1))
                at_least(pe, exp_done, s.times(2 * NT, 2 * j + half - 1))
                bank = scores[0:KP, half, 0:HALF]
                pe.matmul(bank, cT_hi[:, b2, kv], g_lo[:, b2, cols], start=True, stop=False)
                pe.matmul(bank, cT_lo[:, b2, kv], g_hi[:, b2, cols], start=False, stop=False)
                pe.matmul(bank, cT_hi[0:DC, b2, kv], g_hi[:, b2, cols], start=False, stop=True)\
                    .then_inc(scores_full, 1)

            def p_times_c(s, j, t0_off=0):
                b2 = (s.t0 + t0_off) % 2
                pe.wait_ge(exp_done, s.times(2 * NT, 2 * NT * t0_off + 2 * j + 2))
                n_dve = sum(jj <= j for jj, _ in LO_DVE)
                n_pool = sum(jj <= j for jj, _ in LO_POOL)
                at_least(pe, lo_dve, s.times(len(LO_DVE), len(LO_DVE) * t0_off + n_dve))
                pe.wait_ge(lo_pool, s.times(len(LO_POOL), len(LO_POOL) * t0_off + n_pool))
                if j == 0:
                    pe.wait_ge(c_lo_done, s.times(1, 1 + t0_off))
                    at_least(pe, u_part_done, s.times(2, 2 * t0_off))
                for r in range(NR):
                    rows = slice(r * 128, (r + 1) * 128)
                    acc = pc[:, r % 4, (r // 4) * CN:(r // 4 + 1) * CN]
                    pe.matmul(acc, prob_hi[:, j % NPB, rows], cn[:, b2, j, 0:CN],
                              start=(j == 0 and r < 4), stop=False, skip_group_check=True)
                    mm = pe.matmul(acc[:, 0:DC + 1], prob_lo[:, j % NPB, rows], cn[:, b2, j, 0:DC + 1],
                                   start=False, stop=(j == NT - 1), skip_group_check=True)
                mm.then_inc(pc_done, 1)

            def step(s):
                for j in range(NT):
                    side_work(s, j, 0)
                    second_pass(s, j, 0)
                    side_work(s, j, 1)
                    second_pass(s, j, 1)
                    side_work(s, j, 2)
                    if j >= LAG:
                        p_times_c(s, j - LAG)
                    elif s.t0 > 0:
                        p_times_c(s, NT - LAG + j, -1)

            pe.wait_ge(const_ready, 1)
            pe.wait_ge(wq_loaded, 16)
            for b in range(2):
                for i in range(4):
                    blk = 4 * b + i
                    mm = pe.transpose(pc[:, b, i * D:(i + 1) * D], wq[:, blk * 128:(blk + 1) * 128], ident[:, :])
                mm.then_inc(w_full, 1)
            pe.wait_ge(wk_loaded, 16)
            for b in range(2):
                for i in range(4):
                    blk = 4 * b + i
                    mm = pe.transpose(pc[:, 2 + b, i * DC:(i + 1) * DC], wk[:, blk * 128:(blk + 1) * 128],
                                      ident[0:DC, 0:DC])
                mm.then_inc(w_full, 1)
            for p in range(NP):
                pe.wait_ge(ln_step, LN_XN + p + 1)
                mm = pe.transpose(scores[:, 0, p * PAIR:(p + 1) * PAIR], xn[:, p, :], ident[0:PAIR, 0:PAIR])
            mm.then_inc(xnT_full, 1)
            pro = Prologue()
            for k in range(3):
                transpose_c(pro, k, k)

            def products(banks, eight, left, right, width):
                for i in range(4):
                    for odd, bank in enumerate(banks):
                        part = slice(DH * odd, DH * odd + DH)
                        mm = pe.matmul(bank[:, i * width:(i + 1) * width], left[part, 4 * eight + i, :],
                                       right[part, 4 * eight + i, :], start=True, stop=True)
                        if i == 3:
                            mm.then_inc(w_full, 1)

            pe.wait_ge(w_taken, 2)
            pe.wait_ge(wk_taken, 2)
            products([scores[:, 1], pc[:, 0]], 0, wqT, wkT, DC)
            products([pc[:, 1], pc[:, 2]], 1, wqT, wkT, DC)
            pe.wait_ge(g_ready, 4)
            pe.wait_ge(xnT_ready, 1)
            for k in range(3, 5):
                make_g(pro, k, k - 3)
            for k in range(5, 5 + NR * NC):
                first_pass(pro, k, k - 5)
                if k == 7:
                    pe.wait_ge(wv_loaded, 16)
                    for b in range(2):
                        for i in range(4):
                            blk = 4 * b + i
                            mm = pe.transpose(pc[:, 2 + b, i * DC:(i + 1) * DC],
                                              wv[:, blk * 128:(blk + 1) * 128], ident[0:DC, 0:DC])
                        mm.then_inc(w_full, 1)
                if k == 12:
                    pe.wait_ge(w_taken, 4)
                    pe.wait_ge(wo_loaded, 16)
                    products([pc[0:DC, 0], pc[0:DC, 1]], 0, wvT, wo, D)
                    products([pc[0:DC, 2], pc[0:DC, 3]], 1, wvT, wo, D)
            pe.wait_ge(late_const, 5)
            turn_max(pro, 26, 0)
            turn_max(pro, 27, 1)
            pe.wait_ge(w_taken, 8)
            run_steps(pe, step)
            s = Step(B, TAIL)
            for j in range(NT - LAG, NT):
                p_times_c(s, j, -1)
            for k, (what, m, _, _) in enumerate(TAIL):
                WORK[what](s, k, m)

        @block.scalar
        def _(act):
            act.dma_start(wq[:, :], w_q).then_inc(wq_loaded, 16)
            act.dma_start(bias[:, :], b_out.rearrange("(a n) -> a n", a=1).to_broadcast([PAIR, D]))\
                .then_inc(bias_loaded, 16)

            def ct_hi(s, k, c):
                act.wait_ge(ct_full, s.times(NC, NC + c + 1))
                act.activation(cT_hi[0:DC, (s.t0 + 1) % 2, c * CW:(c + 1) * CW], side[0:DC, k % 2, 0:CW],
                               ACT.Copy).then_inc(ct_hi_done, 1)

            def g_hi_half(s, k, half):
                act.wait_ge(g_full, s.times(2, 2 + half + 1))
                act.activation(g_hi[:, (s.t0 + 1) % 2, half * HALF:(half + 1) * HALF],
                               side[0:DC, k % 2, 0:HALF], ACT.Copy).then_inc(g_hi_done, 1)

            def max_row(s, k, m):
                act.wait_ge(mrow_full, s.times(2, 2 + m + 1))
                w = 512 if m == 0 else ROWS - 512
                act.activation(g_lo[DC:DC + 1, (s.t0 + 1) % 2, 512 * m:512 * m + w],
                               side[DC:DC + 1, k % 2, 0:w], ACT.Copy).then_inc(side_free[k % 2], 1)

            def u_turned(s, k, m):
                act.wait_ge(ut_full, s.times(2, -2 + m + 1))
                e2, split = (s.t0 - 1) % 2, 512 // Q
                rest = 512 % Q
                if m == 0:
                    act.activation(uT[:, split, e2, 0:rest], side[0:DC, k % 2, split * Q:512], ACT.Copy)
                    heads, whole = slice(0, split), side[0:DC, k % 2, 0:split * Q]
                else:
                    act.activation(uT[:, split, e2, rest:Q], side[0:DC, k % 2, 0:Q - rest], ACT.Copy)
                    heads, whole = slice(split + 1, H), side[0:DC, k % 2, Q - rest:ROWS - 512]
                act.activation(uT[:, heads, e2, :], whole.rearrange("c (h q) -> c h q", q=Q),
                               ACT.Copy).then_inc(side_free[k % 2], 1)

            def rhs_out(s, k, m):
                if m == 1:
                    act.wait_ge(rhs_full, 2)
                    act.activation(rhs_i[:, :], side[:, k % 2, 0:D // 2].bitcast(F16), ACT.Copy)
                    act.activation(rhs_row[:, :], side[0:PAIR, k % 2, D:2 * D], ACT.Copy)\
                        .then_inc(side_free[k % 2], 1)

            WORK = {"ct": ct_hi, "g": g_hi_half, "mrow": max_row, "ut": u_turned, "rhs": rhs_out}

            def side_work(s, j, place):
                for k, what, m in at(s.schedule, j, place):
                    if what in WORK:
                        WORK[what](s, k, m)

            def exp_half(s, j, half):
                act.wait_ge(scores_full, s.times(2 * NT, 2 * j + half + 1))
                at_least(act, pc_done, s.times(NT, j - NPB + 1))
                act.activation(prob[:, j % NPB, half * HALF:(half + 1) * HALF], scores[0:KP, half, 0:HALF],
                               ACT.Exp).then_inc(exp_done, 1)

            def split_c(s):
                n2 = (s.t0 + 1) % 2
                at_least(act, c_loaded[n2], s.times(8, 24 if not n2 else 16))
                at_least(act, pc_done, s.times(NT))
                act.activation(cn[:, n2, :, 0:DC], c32[:, n2], ACT.Copy).then_inc(c_hi_done, 1)

            def step(s):
                for j in range(NT):
                    side_work(s, j, 0)
                    exp_half(s, j, 0)
                    side_work(s, j, 1)
                    exp_half(s, j, 1)
                    side_work(s, j, 2)
                    if j == 2 and s.t0 < B - 1:
                        split_c(s)

            for b in range(2):
                act.wait_ge(w_full, b + 1)
                act.activation(wqT[:, 4 * b:4 * b + 4, :], pc[:, b, 0:4 * D], ACT.Copy).then_inc(w_taken, 1)
            pro = Prologue()
            for k in range(3):
                ct_hi(pro, k, k)
            act.wait_ge(xnT_full, 1)
            act.activation(xnT[:, :], scores[:, 0, 0:B * Q], ACT.Copy).then_inc(xnT_ready, 1)
            for four in range(2):
                act.wait_ge(w_full, 5 + four)
                bank = scores[:, 1] if four == 0 else pc[:, 0]
                act.activation(G[:, four:8:2, :], bank[:, 0:4 * DC].rearrange("p (h c) -> p h c", h=4),
                               ACT.Copy, scale=SCALE).then_inc(g_ready, 1)
            for k in range(3, 5):
                g_hi_half(pro, k, k - 3)
            at_least(act, c_loaded[0], 16)
            act.activation(cn[:, 0, :, 0:DC], c32[:, 0], ACT.Copy).then_inc(c_hi_done, 1)
            for b in range(2):
                act.wait_ge(w_full, 9 + b)
                act.activation(wvT[:, 4 * b:4 * b + 4, :], pc[:, 2 + b, 0:4 * DC], ACT.Copy).then_inc(w_taken, 1)
            for four in range(4):
                act.wait_ge(w_full, 11 + four)
                first = 8 * (four // 2) + four % 2
                act.activation(M[:, first:first + 7:2, :],
                               pc[0:DC, four, 0:4 * D].rearrange("p (h c) -> p h c", h=4), ACT.Copy)\
                    .then_inc(w_taken, 1)
            max_row(pro, 26, 0)
            max_row(pro, 27, 1)
            run_steps(act, step)
            s = Step(B, TAIL)
            for m in range(2):
                u_turned(s, m, m)

        @block.vector
        def _(dve):
            def ct_lo(s, k, c):
                n2 = (s.t0 + 1) % 2
                cols = slice(c * CW, (c + 1) * CW)
                dve.wait_ge(ct_hi_done, s.times(NC, NC + c + 1))
                dve.tensor_tensor(cT_lo[:, n2, cols], side[0:DC, k % 2, 0:CW], cT_hi[0:DC, n2, cols],
                                  ALU.subtract).then_inc(side_free[k % 2], 1)

            def g_lo_half(s, k, half):
                n2 = (s.t0 + 1) % 2
                cols = slice(half * HALF, (half + 1) * HALF)
                dve.wait_ge(g_hi_done, s.times(2, 2 + half + 1))
                dve.tensor_tensor(g_lo[0:DC, n2, cols], side[0:DC, k % 2, 0:HALF], g_hi[:, n2, cols],
                                  ALU.subtract).then_inc(side_free[k % 2], 1)

            def chunk_max(s, k, m):
                dve.wait_ge(max_full, s.times(NR * NC, NR * NC + m + 1))
                dve.tensor_reduce(maxes[:, m // NC, m % NC:m % NC + 1], side[:, k % 2, 0:CW], AX.X,
                                  ALU.max).then_inc(side_free[k % 2], 1)
                if m == NR * NC - 1:
                    dve.wait_ge(side_free[k % 2], s.freed(k + 2))
                    at_least(dve, mrow_full, s.times(2, 2))
                    dve.tensor_reduce(neg_max[:, :], maxes[:, :, :], AX.X, ALU.max,
                                      negate=True).then_inc(neg_max_done, 1)

            def take_u(s):
                dve.wait_ge(pc_done, s.times(NT))
                parts = [(slice(0, 4), pc[:, 0:4, 0:CN]), (slice(4, NR), pc[:, 0:NR - 4, CN:2 * CN])]
                for rows, acc in parts:
                    dve.reciprocal(rsum[:, rows], acc[:, :, DC]).then_inc(rsum_done, 1)
                for n, (rows, acc) in enumerate(parts):
                    dve.wait_ge(rsum_done, s.times(2, -2 + n + 1))
                    count = rows.stop - rows.start
                    dve.tensor_tensor(u_part[:, rows, :], acc,
                                      rsum[:, rows].rearrange("p (r a) -> p r a", a=1).to_broadcast([128, count, CN]),
                                      ALU.mult).then_inc(u_part_done, 1)

            def finish_x1(s, k, m):
                dve.wait_ge(out_full, s.pairs(1, 1))
                if s.i is None:
                    resid = xb[:, s.pairs(1), :]
                else:
                    resid = xb[:, bass.ds(s.pairs(1), 1), :].rearrange("p a d -> p (a d)")
                dve.tensor_tensor(x1[:, :], side[0:PAIR, k % 2, 0:D], resid, ALU.add)\
                    .then_inc(side_free[k % 2], 1)
                dve.wait_ge(side_free[k % 2], s.freed(k + 2))
                dve.bn_stats(st2[:, :], x1[:, :]).then_inc(ffn_step, 1)

            def row_moments(s):
                dve.bn_aggr(mv2[:, :], st2[:, :]).then_inc(ffn_step, 1)
                dve.wait_ge(ffn_step, s.pairs(NFFN, 2))
                dve.tensor_scalar(ve2[:, :], mv2[:, 1:2], EPS, None, ALU.add).then_inc(ffn_step, 1)

            def quantise(s):
                dve.wait_ge(rstd2_done, s.pairs(1, 1))
                dve.tensor_scalar(xn2[:, :], x1[:, :], mv2[:, 0:1], rstd2[:, :], ALU.subtract, ALU.mult)\
                    .then_inc(ffn_step, 1)
                dve.wait_ge(ffn_step, s.pairs(NFFN, 4))
                dve.tensor_reduce(row_sc[:, 0:1], xn2[:, :], AX.X, ALU.max, apply_absolute_value=True)\
                    .then_inc(ffn_step, 1)
                dve.wait_ge(ffn_step, s.pairs(NFFN, 5))
                dve.tensor_scalar(row_sc[:, 1:2], row_sc[:, 0:1], 1e-12, 1.0 / QMAX, ALU.max, ALU.mult)\
                    .then_inc(ffn_step, 1)
                dve.wait_ge(ffn_step, s.pairs(NFFN, 6))
                dve.reciprocal(row_sc[:, 2:3], row_sc[:, 1:2]).then_inc(ffn_step, 1)
                dve.wait_ge(ffn_step, s.pairs(NFFN, 7))
                dve.tensor_scalar(q_a[:, :], xn2[:, :], row_sc[:, 2:3], QMAX, ALU.mult, ALU.min)\
                    .then_inc(ffn_step, 1)
                dve.wait_ge(ffn_step, s.pairs(NFFN, 8))
                dve.tensor_scalar(q_b[:, :], q_a[:, :], -QMAX, ROUND, ALU.max, ALU.add).then_inc(ffn_step, 1)
                dve.wait_ge(ffn_step, s.pairs(NFFN, 9))
                dve.tensor_scalar(q_i[:, :], q_b[:, :], ROUND, None, ALU.subtract).then_inc(ffn_step, 1)

            def take_qT(s, k, m):
                dve.wait_ge(ft_full, s.pairs(1, 1))
                dve.tensor_copy(q_iT[:, :], side[:, k % 2, 0:PAIR // 2].bitcast(F16))\
                    .then_inc(side_free[k % 2], 1)

            def finish_pair(s, k, m):
                dve.wait_ge(fm_full, s.pairs(1, 1))
                dve.scalar_tensor_tensor(out=y_a[:, :], in0=side[0:PAIR, k % 2, 0:D], scalar=row_sc[:, 1:2],
                                         in1=rhs_row[:, :], op0=ALU.mult, op1=ALU.mult)\
                    .then_inc(side_free[k % 2], 1)
                dve.wait_ge(side_free[k % 2], s.freed(k + 2))
                if s.i is None:
                    y_pair = y[:, s.pairs(1), :]
                else:
                    y_pair = y[:, bass.ds(s.pairs(1), 1), :].rearrange("p a d -> p (a d)")
                dve.tensor_tensor(y_pair, y_a[:, :], x1[:, :], ALU.add).then_inc(y_done, 1)

            def rhs_quantise(s, k, m):
                if m != 0:
                    return
                dve.wait_ge(rhs_full, 1)
                rt = side[:, k % 2, 0:D]
                dve.tensor_reduce(rhs_sc[:, 0:1], rt, AX.X, ALU.max, apply_absolute_value=True)\
                    .then_inc(rhs_step, 1)
                dve.wait_ge(rhs_step, 1)
                dve.tensor_scalar(rhs_sc[:, 1:2], rhs_sc[:, 0:1], 1e-12, 1.0 / QMAX, ALU.max, ALU.mult)\
                    .then_inc(rhs_step, 1)
                dve.wait_ge(rhs_step, 2)
                dve.reciprocal(rhs_sc[:, 2:3], rhs_sc[:, 1:2]).then_inc(rhs_step, 1)
                dve.wait_ge(rhs_step, 3)
                dve.tensor_scalar(rhs_diag[:, :], rt, rhs_sc[:, 2:3], QMAX, ALU.mult, ALU.min)\
                    .then_inc(side_free[k % 2], 1)
                dve.wait_ge(side_free[k % 2], s.freed(k + 2))
                dve.tensor_scalar(rhsT_q[:, :], rhs_diag[:, :], -QMAX, ROUND, ALU.max, ALU.add)\
                    .then_inc(rhs_step, 1)
                dve.wait_ge(rhs_step, 4)
                dve.tensor_scalar(rhsT_i[:, :], rhsT_q[:, :], ROUND, None, ALU.subtract).then_inc(rhs_step, 1)
                dve.tensor_scalar(rhs_diag[:, :], ident[:, :], rhs_sc[:, 1:2], None, ALU.mult)\
                    .then_inc(rhs_step, 1)

            WORK = {"ct": ct_lo, "g": g_lo_half, "max": chunk_max, "out": finish_x1, "ft": take_qT,
                    "fm": finish_pair, "rhs": rhs_quantise}

            def side_work(s, j, place):
                for k, what, m in at(s.schedule, j, place):
                    if what in WORK:
                        WORK[what](s, k, m)

            def prob_low(s, j, half):
                dve.wait_ge(exp_done, s.times(2 * NT, 2 * j + half + 1))
                cols = slice(half * HALF, (half + 1) * HALF)
                dve.tensor_tensor(prob_lo[:, j % NPB, cols], prob[:, j % NPB, cols], prob_hi[:, j % NPB, cols],
                                  ALU.subtract).then_inc(lo_dve, 1)

            def step(s):
                for j in range(NT):
                    if j == 2 and s.t0 > 0:
                        take_u(s)
                    if j == 7 and s.t0 > 0 and not s.odd:
                        quantise(s)
                    side_work(s, j, 0)
                    side_work(s, j, 1)
                    moments = j == 5 and s.t0 > 0 and not s.odd
                    if moments:
                        dve.wait_ge(ffn_step, s.pairs(NFFN, 1))
                    if (j, 0) in LO_DVE:
                        prob_low(s, j, 0)
                    if moments:
                        row_moments(s)
                    side_work(s, j, 2)

            dve.memset(minus_half[:, :], -0.5).then_inc(minus_half_ready, 1)
            dve.memset(cn[:, :, :, DC:DC + 1], 1.0).then_inc(late_const, 1)
            dve.memset(cT_hi[DC:DC + 1, 0, :], 1.0).then_inc(late_const, 1)
            dve.wait_ge(x_loaded, 16)
            for p in range(NP):
                dve.bn_stats(st1[:, p, :], x_in[:, p, :]).then_inc(ln_step, 1)
            for p in range(NP):
                dve.wait_ge(ln_step, p + 1)
                dve.bn_aggr(mv1[:, p, :], st1[:, p, :]).then_inc(ln_step, 1)
            dve.wait_ge(ln_step, 2 * NP)
            dve.tensor_scalar(ve1[:, :], mv1[:, :, 1], EPS, None, ALU.add).then_inc(ln_step, 1)
            for b in range(2):
                dve.wait_ge(w_full, 3 + b)
                dve.tensor_copy(wkT[:, 4 * b:4 * b + 4, :].rearrange("p a c -> p (a c)"), pc[:, 2 + b, 0:4 * DC])\
                    .then_inc(wk_taken, 1)
            dve.wait_ge(ln_rstd, 1)
            for p in range(NP):
                dve.tensor_scalar(xn[:, p, :], x_in[:, p, :], mv1[:, p, 0:1], rstd1[:, p:p + 1],
                                  ALU.subtract, ALU.mult).then_inc(ln_step, 1)
            pro = Prologue()
            for k in range(3):
                ct_lo(pro, k, k)
            for four in range(2, 4):
                dve.wait_ge(w_full, 5 + four)
                dve.tensor_scalar(G[:, 6 + four:H:2, :],
                                  pc[:, four - 1, 0:4 * DC].rearrange("p (h c) -> p h c", h=4),
                                  SCALE, None, ALU.mult).then_inc(g_ready, 1)
            for k in range(3, 5):
                g_lo_half(pro, k, k - 3)
            for k in range(5, 5 + NR * NC):
                chunk_max(pro, k, k - 5)
            dve.memset(cT_hi[DC:DC + 1, 1, :], 1.0).then_inc(late_const, 1)
            dve.wait_ge(bias_loaded, 16)
            dve.tensor_tensor(xb[:, :, :], x_in[:, :, :],
                              bias[:, :].rearrange("p (a d) -> p a d", a=1).to_broadcast([PAIR, NP, D]),
                              ALU.add).then_inc(xb_ready, 1)
            dve.wait_ge(xb_ready, 1)
            run_steps(dve, step)
            s = Step(B, TAIL)
            take_u(s)
            finish_x1(s, 2, 0)
            dve.wait_ge(ffn_step, s.pairs(NFFN, 1))
            row_moments(s)
            quantise(s)
            take_qT(s, 3, 0)
            finish_pair(s, 4, 0)

        @block.gpsimd
        def _(pool):
            def prob_low(s, j, half):
                pool.wait_ge(exp_done, s.times(2 * NT, 2 * j + half + 1))
                cols = slice(half * HALF, (half + 1) * HALF)
                pool.tensor_tensor(prob_lo[:, j % NPB, cols], prob[:, j % NPB, cols], prob_hi[:, j % NPB, cols],
                                   ALU.subtract).then_inc(lo_pool, 1)

            def add_u(s):
                pool.wait_ge(u_part_done, s.times(2))
                at_least(pool, ut_full, s.times(2, -2))
                pool.tensor_tensor(u[:, :, :], u_part[:, :, 0:DC], u_part[:, :, DC + 1:CN],
                                   ALU.add).then_inc(u_done, 1)

            def split_c(s):
                n2 = (s.t0 + 1) % 2
                pool.wait_ge(c_hi_done, s.times(1, 2))
                pool.tensor_tensor(cn[:, n2, :, DC + 1:CN], c32[:, n2], cn[:, n2, :, 0:DC],
                                   ALU.subtract).then_inc(c_lo_done, 1)

            def row_std(s):
                pool.wait_ge(ffn_step, s.pairs(NFFN, 3))
                pool.tensor_tensor(rstd2[:, :], ve2[:, :], minus_half[0:PAIR, 0:1], ALU.pow)\
                    .then_inc(rstd2_done, 1)

            def step(s):
                for j in range(NT):
                    if j == 3 and s.t0 > 0:
                        add_u(s)
                    if j == 4 and s.t0 < B - 1:
                        split_c(s)
                    if j == 7 and s.t0 > 0 and not s.odd:
                        row_std(s)
                    for h in (1, 0):
                        if (j, h) in LO_POOL:
                            prob_low(s, j, h)

            pool.memset(ident[:, :], 0.0).then_inc(const_step, 1)
            pool.wait_ge(const_step, 1)
            pool.affine_select(out=ident[:, :], in_=ident[:, :], compare_op=ALU.not_equal, fill=1.0, base=0,
                               pattern=[[-1, 128]], channel_multiplier=1).then_inc(const_ready, 1)
            pool.wait_ge(minus_half_ready, 1)
            pool.wait_ge(ln_step, 2 * NP + 1)
            pool.tensor_tensor(rstd1[:, :], ve1[:, :], minus_half[0:PAIR, :], ALU.pow).then_inc(ln_rstd, 1)
            pool.wait_ge(const_ready, 1)
            pool.tensor_copy(ident16[:, :], ident[:, :]).then_inc(late_const, 1)
            pool.memset(ones[:, :], 1.0).then_inc(late_const, 1)
            split_c(Prologue())
            run_steps(pool, step)
            s = Step(B, TAIL)
            add_u(s)
            row_std(s)


_INS = ["x", "ctx_768", "L0_xattn_w_q", "L0_xattn_w_k", "L0_xattn_w_v", "L0_xattn_w_out", "L0_xattn_b_out",
        "L0_ffn_rhs"]


def kernel(**inputs):
    import numpy as _np
    import concourse.bacc as _bacc
    from concourse import mybir as _mybir
    from concourse.bass_utils import run_bass_kernel_spmd as _run

    nc = _bacc.Bacc("TRN2", target_bir_lowering=False, num_devices=1)
    arrays, args = {}, []
    for name in _INS:
        a = _np.ascontiguousarray(inputs[name])
        arrays[f"in_{name}"] = a
        args.append(nc.dram_tensor(f"in_{name}", a.shape, _mybir.dt.from_np(a.dtype), kind="ExternalInput").ap())
    args.append(nc.dram_tensor("out_y", (B, Q, D), F32, kind="ExternalOutput").ap())
    build(nc, *args)
    r = _run(nc, [arrays], core_ids=[0])
    return r.results[0]["out_y"]
```

```python
from contextlib import ExitStack

import concourse.bass as bass
from concourse import mybir

F32 = mybir.dt.float32
F16 = mybir.dt.float16
BF16 = mybir.dt.bfloat16
ALU = mybir.AluOpType
ACT = mybir.ActivationFunctionType
AX = mybir.AxisListType

B, Q, D = 8, 56, 128
KV, DC = 1500, 96
H, DH = 16, 64
KP = 125
NT = KV // KP
ROWS = H * Q
HALF = ROWS // 2
NR = ROWS // 128
NC = 3
TC = NT // NC
CW = KV // NC
CN = 2 * DC + 1
PAIR = 2 * Q
NP = B // 2
HG = H // 2
LAG = 2
NPB = 4
G_UP = 16.0
G_DOWN = DH ** -0.5 / G_UP
EPS = 1e-5
QMAX = 127.0
ROUND = 1.5 * 2.0 ** 23
WARM_UP = 10
NFFN = 10

TILES = [(j, h) for j in range(NT) for h in (0, 1)]
LO_DVE = [(j, h) for j, h in TILES if h == 0 and j % 3 != 1]
LO_DVE_LAST = [(j, h) for j, h in TILES if h == 0 or j % 2 == 1]

PREP_HEAD = [(0, 0, "ct", 0), (0, 1, "ct", 1), (1, 0, "ct", 2), (1, 1, "g", 0), (2, 0, "g", 1)]
UT = [(4, 0, "ut", 0), (4, 1, "ut", 1)]
RHS = [(4, 0, "rhs", 0), (6, 0, "rhs", 1)]
OUT = [(5, 0, "out", 0), (5, 2, "out", 1), (10, 1, "ft", 0), (11, 0, "fm", 0)]
MAX_AT = [(3, 0), (3, 1), (3, 2), (4, 2), (5, 1), (5, 2), (6, 0), (6, 1), (6, 2), (7, 0), (7, 1),
          (7, 2), (8, 0), (8, 1), (8, 2), (9, 0), (9, 1), (9, 2), (10, 0), (10, 1), (10, 2)]
MAXES = [(j, a, "max", m) for m, (j, a) in enumerate(MAX_AT)]
MROW = [(8, 2, "mrow", 0), (11, 1, "mrow", 1)]
MROW_AFTER = [3 * NC + 2, NR * NC - 1]


EIGHT_HEADS = [slice(0, 8, 2), slice(1, 8, 2), slice(8, H, 2), slice(9, H, 2)]
G_BANKS = [-1, 2, 3, 1]
M_BANKS = [0, 3, 2, 0]


def in_order(*lists):
    return [(what, m, j, a) for j, a, _, what, m in
            sorted((j, a, n, what, m) for n, l in enumerate(lists) for j, a, what, m in l)]


def prepare():
    yield from (("ct", 0), ("ct", 1), ("ct", 2), ("g", 0), ("g", 1))
    for m in range(NR * NC):
        yield "max", m
        if m == MROW_AFTER[0] + 2:
            yield "mrow", 0
    yield "mrow", 1


PREP = [(what, m, 0, 0) for what, m in prepare()]
FIRST = in_order(RHS, PREP_HEAD, MAXES, MROW)
ODD = in_order(UT, PREP_HEAD, MAXES, MROW)
EVEN = in_order(OUT, UT, PREP_HEAD, MAXES, MROW)
LAST = in_order(UT)
TAIL = [("ut", 0, 0, 0), ("ut", 1, 0, 0), ("out", 0, 0, 0), ("out", 1, 0, 0), ("ft", 0, 0, 0), ("fm", 0, 0, 0)]
assert all(len(s) % 2 == 0 for s in (PREP, FIRST, ODD, EVEN, LAST, TAIL))


def uses(schedule, bank):
    return (len(schedule) + 1 - bank) // 2


class Step:

    def __init__(self, t0, schedule, i=None):
        self.t0, self.i, self.schedule = t0, i, schedule
        self.odd = t0 % 2

    def times(self, per, more=0):
        fixed = per * self.t0 + more
        return fixed if self.i is None else self.i * (2 * per) + fixed

    def pairs(self, per, more=0):
        fixed = per * ((self.t0 - 1) // 2) + more
        return fixed if self.i is None else self.i * per + fixed

    def freed(self, k):
        bank = k % 2
        fixed = uses(PREP, bank) + k // 2
        if self.t0 > 0:
            fixed += uses(FIRST, bank)
        if self.i is not None:
            if not self.odd:
                fixed += uses(ODD, bank)
            return self.i * (uses(ODD, bank) + uses(EVEN, bank)) + fixed
        if self.t0 > 0:
            fixed += 3 * (uses(ODD, bank) + uses(EVEN, bank))
        if self.t0 > B - 1:
            fixed += uses(LAST, bank)
        return fixed


class Prologue(Step):

    def __init__(self):
        super().__init__(-1, PREP)
        self.odd = 1

    def freed(self, k):
        return k // 2


def low_parts(batch):
    by_dve = LO_DVE_LAST if batch == B - 1 else LO_DVE
    return by_dve, [jh for jh in TILES if jh not in by_dve]


def at_least(eng, sem, value):
    if not isinstance(value, int) or value > 0:
        eng.wait_ge(sem, value)


def run_steps(eng, step):
    step(Step(0, FIRST))
    with eng.Fori(0, (B - 2) // 2) as i:
        step(Step(1, ODD, i))
        step(Step(2, EVEN, i))
    step(Step(B - 1, LAST))


def use_of(schedule, what, m):
    return [k for k, use in enumerate(schedule) if use[:2] == (what, m)][0]


def at(schedule, j, place):
    return [(k, what, m) for k, (what, m, jj, a) in enumerate(schedule) if (jj, a) == (j, place)]


def build(nc, x, ctx_kv, w_q, w_k, w_v, w_out, b_out, rhs, out):
    with ExitStack() as stack:
        def sb(name, shape, dt):
            return stack.enter_context(nc.sbuf_tensor(name, shape, dt))

        def psum(name, shape, dt):
            return stack.enter_context(nc.psum_tensor(name, shape, dt))

        def sem(name):
            return stack.enter_context(nc.semaphore(name))

        scores = psum("scores", [128, 2, 512], F32)
        side = psum("side", [128, 2, 512], F32)
        pc = psum("pc", [128, 4, 512], F32)

        ident = sb("ident", [128, 128], F32)
        ident16 = sb("ident16", [128, 128], F16)
        ones = sb("ones", [128, PAIR], F32)
        minus_half = sb("minus_half", [128, NP], F32)
        wq = sb("wq", [D, H * DH], F32)
        wk = sb("wk", [DC, H * DH], F32)
        wv = sb("wv", [DC, H * DH], F32)
        wo = sb("wo", [128, H // 2, D], F32)
        wqT = sb("wqT", [128, H // 2, D], F32)
        wkT = sb("wkT", [128, H // 2, DC], F32)
        wvT = sb("wvT", [128, H, DC], F32)
        G_hi = sb("G_hi", [D, H, DC], F16)
        G_lo = sb("G_lo", [D, H, DC], F16)
        M = sb("M", [DC, H, D], F32)
        bias = sb("bias", [PAIR, D], F32)
        rhs_in = sb("rhs_in", [D, D], F32)
        rhsT_q = sb("rhsT_q", [D, D], F32)
        rhsT_i = sb("rhsT_i", [D, D], F16)
        rhs_i = sb("rhs_i", [D, D], F16)
        rhs_sc = sb("rhs_sc", [D, 4], F32)
        rhs_diag = sb("rhs_diag", [D, D], F32)
        rhs_row = sb("rhs_row", [PAIR, D], F32)

        x_in = sb("x_in", [PAIR, NP, D], F32)
        xn = sb("xn", [PAIR, NP, D], F32)
        xb = sb("xb", [PAIR, NP, D], F32)
        xnT_hi = sb("xnT_hi", [D, B * Q], F16)
        xnT_lo = sb("xnT_lo", [D, B * Q], F16)
        st1 = sb("st1", [PAIR, NP, 6], F32)
        mv1 = sb("mv1", [PAIR, NP, 2], F32)
        ve1 = sb("ve1", [PAIR, NP], F32)
        rstd1 = sb("rstd1", [PAIR, NP], F32)

        c32 = sb("c32", [KP, 2, NT, DC], F32)
        cn = sb("cn", [KP, 2, NT, CN + 1], F16)
        cT_hi = sb("cT_hi", [DC + 1, 2, KV], F16)
        cT_lo = sb("cT_lo", [DC, 2, KV], F16)
        g_hi = sb("g_hi", [DC, 2, ROWS], F16)
        g_lo = sb("g_lo", [DC + 1, 2, ROWS], F16)
        maxes = sb("maxes", [128, NR, NC], F32)
        neg_max = sb("neg_max", [128, NR], F16)
        prob = sb("prob", [KP, NPB, ROWS], F32)
        prob_lo = sb("prob_lo", [KP, NPB, ROWS], F16)
        rsum = sb("rsum", [128, NR], F32)
        u_part = sb("u_part", [128, NR, CN], F32)
        u = sb("u", [128, NR, DC], F32)
        uT = sb("uT", [DC, H, 2, Q], F32)

        x1_part = sb("x1_part", [PAIR, D], F32)
        x1 = sb("x1", [PAIR, D], F32)
        st2 = sb("st2", [PAIR, 6], F32)
        mv2 = sb("mv2", [PAIR, 2], F32)
        ve2 = sb("ve2", [PAIR, 1], F32)
        rstd2 = sb("rstd2", [PAIR, 1], F32)
        xn2 = sb("xn2", [PAIR, D], F32)
        row_sc = sb("row_sc", [PAIR, 3], F32)
        q_a = sb("q_a", [PAIR, D], F32)
        q_b = sb("q_b", [PAIR, D], F32)
        q_i = sb("q_i", [PAIR, D], F16)
        q_iT = sb("q_iT", [D, PAIR], F16)
        y_a = sb("y_a", [PAIR, D], F32)
        y = sb("y", [PAIR, NP, D], F32)

        prob_hi = prob[:, :, :].bitcast(BF16).rearrange("p b (n two) -> p b n two", two=2)[:, :, :, 1]

        x_loaded, x_rest_loaded = sem("x_loaded"), sem("x_rest_loaded")
        wq_loaded, wk_loaded = sem("wq_loaded"), sem("wk_loaded")
        wv_loaded, wo_loaded, rhs_loaded = sem("wv_loaded"), sem("wo_loaded"), sem("rhs_loaded")
        bias_loaded = sem("bias_loaded")
        c_loaded = [sem("c_loaded_even"), sem("c_loaded_odd")]
        out_stored = sem("out_stored")
        wvT_zeroed, ident16_ready = sem("wvT_zeroed"), sem("ident16_ready")
        ones_ready = sem("ones_ready")
        const_ready = sem("const_ready")
        w_full = sem("w_full")
        w_act, w_dve = sem("w_act"), sem("w_dve")
        G_hi_done, G_lo_done = sem("G_hi_done"), sem("G_lo_done")
        ln_step, ln_rstd, xn_done = sem("ln_step"), sem("ln_rstd"), sem("xn_done")
        xnT_full, xnT_hi_done, xnT_lo_done = sem("xnT_full"), sem("xnT_hi_done"), sem("xnT_lo_done")
        rhs_step = sem("rhs_step")
        const_step, late_const = sem("const_step"), sem("late_const")
        minus_half_ready, xb_ready = sem("minus_half_ready"), sem("xb_ready")
        scores_full = sem("scores_full")
        pc_done = sem("pc_done")
        ct_full, g_full = sem("ct_full"), sem("g_full")
        max_full, mrow_full = sem("max_full"), sem("mrow_full")
        ut_full = sem("ut_full")
        out_full, ft_full, fm_full = sem("out_full"), sem("ft_full"), sem("fm_full")
        rhs_full = sem("rhs_full")
        side_free = [sem("side0_free"), sem("side1_free")]
        exp_done = sem("exp_done")
        ct_hi_done, g_hi_done = sem("ct_hi_done"), sem("g_hi_done")
        c_hi_done = sem("c_hi_done")
        lo_pool = sem("lo_pool")
        c_lo_done = sem("c_lo_done")
        u_done = sem("u_done")
        rstd2_done = sem("rstd2_done")
        lo_dve = sem("lo_dve")
        neg_max_done = sem("neg_max_done")
        rsum_done, u_part_done = sem("rsum_done"), sem("u_part_done")
        ffn_step = sem("ffn_step")
        y_done = sem("y_done")

        block = stack.enter_context(nc.Block())

        c_dram = ctx_kv.rearrange("b (p j) d -> b p j d", j=NT)
        x_dram = x.rearrange("(n two) q d -> (two q) n d", two=2)
        out_dram = out.rearrange("(n two) q d -> n (two q) d", two=2)

        @block.sync
        def _(sp):
            sp.dma_start(x_in[:, 0], x_dram[:, 0]).then_inc(x_loaded, 16)
            sp.dma_start(wk[:, :], w_k).then_inc(wk_loaded, 16)
            sp.dma_start(c32[:, 0], c_dram[0]).then_inc(c_loaded[0], 16)
            sp.dma_start(wv[:, :], w_v).then_inc(wv_loaded, 16)
            sp.dma_start(c32[:, 1], c_dram[1]).then_inc(c_loaded[1], 16)
            sp.dma_start(rhs_in[:, :], rhs).then_inc(rhs_loaded, 16)
            for b in range(2, B):
                sp.wait_ge(ct_full, NC * (b - 1))
                sp.wait_ge(c_lo_done, b - 1)
                sp.dma_start(c32[:, b % 2], c_dram[b]).then_inc(c_loaded[b % 2], 16)
                if b >= 5 and b % 2 == 1:
                    p = (b - 5) // 2
                    sp.wait_ge(y_done, p + 1)
                    sp.dma_start(out_dram[p], y[:, p, :]).then_inc(out_stored, 16)
            for p in range(2, NP):
                sp.wait_ge(y_done, p + 1)
                sp.dma_start(out_dram[p], y[:, p, :]).then_inc(out_stored, 16)
            sp.wait_ge(out_stored, 16 * NP)

        @block.tensor
        def _(pe):
            def side_bank(s, k):
                at_least(pe, side_free[k % 2], s.freed(k))
                return side[:, k % 2]

            def transpose_c(s, k, c):
                n2 = (s.t0 + 1) % 2
                if c == 0:
                    at_least(pe, c_loaded[n2], s.times(8, 24 if not n2 else 16))
                bank = side_bank(s, k)
                for jj in range(TC):
                    mm = pe.transpose(bank[0:DC, jj * KP:(jj + 1) * KP], c32[:, n2, c * TC + jj],
                                      ident[0:KP, 0:KP])
                mm.then_inc(ct_full, 1)

            def make_g(s, k, half):
                if s.t0 == 0 and half == 0:
                    pe.wait_ge(xnT_lo_done, 2)
                bank = side_bank(s, k)
                first = s.times(Q, Q)
                cols = slice(first, first + Q) if s.i is None else bass.ds(first, Q)
                for h in range(HG):
                    part, head = bank[0:DC, h * Q:(h + 1) * Q], half * HG + h
                    pe.matmul(part, G_hi[:, head, :], xnT_hi[:, cols], start=True, stop=False)
                    pe.matmul(part, G_hi[:, head, :], xnT_lo[:, cols], start=False, stop=False)
                    mm = pe.matmul(part, G_lo[:, head, :], xnT_hi[:, cols], start=False, stop=True)
                mm.then_inc(g_full, 1)

            def first_pass(s, k, m):
                n2 = (s.t0 + 1) % 2
                r, c = m // NC, m % NC
                if m == 0:
                    pe.wait_ge(ct_hi_done, s.times(NC, 2 * NC))
                    pe.wait_ge(g_hi_done, s.times(2, 3))
                if m == 3 * NC:
                    pe.wait_ge(g_hi_done, s.times(2, 4))
                bank = side_bank(s, k)
                pe.matmul(bank[:, 0:CW], g_hi[:, n2, r * 128:(r + 1) * 128],
                          cT_hi[0:DC, n2, c * CW:(c + 1) * CW], start=True, stop=True).then_inc(max_full, 1)

            def turn_max(s, k, m):
                bank = side_bank(s, k)
                pe.wait_ge(neg_max_done, s.times(2, 3 + m))
                for r in range(4 * m, min(4 * m + 4, NR)):
                    mm = pe.matmul(bank[DC:DC + 1, (r % 4) * 128:(r % 4 + 1) * 128], neg_max[:, r:r + 1],
                                   ident16[:, :], start=True, stop=True)
                mm.then_inc(mrow_full, 1)

            def turn_u(s, k, m):
                bank = side_bank(s, k)
                if m == 0:
                    pe.wait_ge(u_done, s.times(1))
                for r in range(4 * m, min(4 * m + 4, NR)):
                    mm = pe.transpose(bank[0:DC, (r % 4) * 128:(r % 4 + 1) * 128], u[:, r, :], ident[:, :])
                mm.then_inc(ut_full, 1)

            def project_out(s, k, m):
                bank = side_bank(s, k)
                pe.wait_ge(side_free[(k + 1) % 2], s.freed(k + 1))
                for h in range(HG):
                    mm = pe.matmul(bank[0:PAIR, 0:D], uT[:, m * HG + h].rearrange("c b q -> c (b q)"),
                                   M[:, m * HG + h, :], start=(h == 0), stop=(h == HG - 1))
                mm.then_inc(out_full, 1)

            def turn_q(s, k, m):
                bank = side_bank(s, k)
                pe.wait_ge(ffn_step, s.pairs(NFFN, NFFN))
                pe.transpose(bank[:, 0:PAIR // 2].bitcast(F16), q_i[:, :],
                             ident16[0:PAIR, 0:PAIR]).then_inc(ft_full, 1)

            def linear(s, k, m):
                bank = side_bank(s, k)
                kt = [kk for kk, use in enumerate(s.schedule) if use[0] == "ft"][0]
                pe.wait_ge(side_free[kt % 2], s.freed(kt + 2))
                pe.matmul(bank[0:PAIR, 0:D], q_iT[:, :], rhs_i[:, :], start=True, stop=True)\
                    .then_inc(fm_full, 1)

            def rhs_work(s, k, m):
                bank = side_bank(s, k)
                if m == 0:
                    pe.wait_ge(rhs_loaded, 16)
                    pe.transpose(bank[:, 0:D], rhs_in[:, :], ident[:, :]).then_inc(rhs_full, 1)
                else:
                    pe.wait_ge(rhs_step, 6)
                    pe.transpose(bank[:, 0:D // 2].bitcast(F16), rhsT_i[:, :], ident16[:, :])
                    pe.matmul(bank[0:PAIR, D:2 * D], ones[:, :], rhs_diag[:, :], start=True, stop=True)\
                        .then_inc(rhs_full, 1)

            WORK = {"ct": transpose_c, "g": make_g, "max": first_pass, "mrow": turn_max, "ut": turn_u,
                    "out": project_out, "ft": turn_q, "fm": linear, "rhs": rhs_work}

            def side_work(s, j, place):
                for k, what, m in at(s.schedule, j, place):
                    WORK[what](s, k, m)

            def second_pass(s, j, half):
                b2 = s.t0 % 2
                kv = slice(j * KP, (j + 1) * KP)
                cols = slice(half * HALF, (half + 1) * HALF)
                if j == 0:
                    before = PREP if s.t0 == 0 else FIRST if s.t0 == 1 and s.i is None else \
                        ODD if s.t0 == 2 else EVEN
                    km = use_of(before, "mrow", half)
                    later = len([k for k in range(km + 2, len(before), 2)])
                    pe.wait_ge(side_free[km % 2], s.freed(km % 2) - later)
                at_least(pe, exp_done, s.times(2 * NT, 2 * j + half - 1))
                bank = scores[0:KP, half, 0:HALF]
                pe.matmul(bank, cT_hi[:, b2, kv], g_lo[:, b2, cols], start=True, stop=False)
                pe.matmul(bank, cT_lo[:, b2, kv], g_hi[:, b2, cols], start=False, stop=False)
                pe.matmul(bank, cT_hi[0:DC, b2, kv], g_hi[:, b2, cols], start=False, stop=True)\
                    .then_inc(scores_full, 1)

            def p_times_c(s, j, t0_off=0):
                b2 = (s.t0 + t0_off) % 2
                pe.wait_ge(exp_done, s.times(2 * NT, 2 * NT * t0_off + 2 * j + 2))
                for sem_lo, mine, usual in zip((lo_dve, lo_pool), low_parts(s.t0 + t0_off), low_parts(0)):
                    upto = sum(jj <= j for jj, _ in mine)
                    at_least(pe, sem_lo, s.times(len(usual), len(usual) * t0_off + upto))
                if j == 0 and s.t0 == 0:
                    pe.wait_ge(w_act, 10)
                    pe.wait_ge(xnT_lo_done, 2)
                if j == 0:
                    pe.wait_ge(c_lo_done, s.times(1, 1 + t0_off))
                    at_least(pe, u_part_done, s.times(2, 2 * t0_off))
                for r in range(NR):
                    rows = slice(r * 128, (r + 1) * 128)
                    acc = pc[:, r % 4, (r // 4) * CN:(r // 4 + 1) * CN]
                    pe.matmul(acc, prob_hi[:, j % NPB, rows], cn[:, b2, j, 0:CN],
                              start=(j == 0 and r < 4), stop=False, skip_group_check=True)
                    mm = pe.matmul(acc[:, 0:DC + 1], prob_lo[:, j % NPB, rows], cn[:, b2, j, 0:DC + 1],
                                   start=False, stop=(j == NT - 1), skip_group_check=True)
                mm.then_inc(pc_done, 1)

            def step(s):
                for j in range(NT):
                    side_work(s, j, 0)
                    second_pass(s, j, 0)
                    side_work(s, j, 1)
                    second_pass(s, j, 1)
                    side_work(s, j, 2)
                    if j >= LAG:
                        p_times_c(s, j - LAG)
                    elif s.t0 > 0:
                        p_times_c(s, NT - LAG + j, -1)

            def turn_weights(w, bank, rows, block, i):
                return pe.transpose(bank[:, i * rows:(i + 1) * rows], w[:, block * 128:(block + 1) * 128],
                                    ident[0:rows, 0:rows])

            def turn_x(p):
                pe.wait_ge(xn_done, p + 1)
                bank = scores[:, 0] if p == 0 else pc[:, 1]
                return pe.transpose(bank[:, p * PAIR:(p + 1) * PAIR], xn[:, p, :], ident[0:PAIR, 0:PAIR])

            def product_g(h):
                b = G_BANKS[h // 8 * 2 + h % 2]
                bank = scores[:, 1] if b < 0 else pc[:, b]
                i, part = h % 8 // 2, slice(DH * (h % 2), DH * (h % 2) + DH)
                mm = pe.matmul(bank[:, i * DC:(i + 1) * DC], wqT[part, h // 2, :], wkT[part, h // 2, :],
                               start=True, stop=True)
                if i == 3:
                    mm.then_inc(w_full, 1)

            def product_m(h):
                bank, i = pc[0:DC, M_BANKS[h // 4]], h % 4
                if h == 12:
                    pe.wait_ge(w_act, 7)
                mm = pe.matmul(bank[:, i * D:(i + 1) * D], wvT[:, h, :], wo[:, h // 2, :], start=True, stop=True)
                if i == 3:
                    mm.then_inc(w_full, 1)

            pro = Prologue()
            def keep_clock_up(products):
                for _ in range(products):
                    pe.matmul(scores[0:PAIR, 1, 0:PAIR], ones[:, :], ones[:, :], start=True, stop=True)

            pe.wait_ge(ones_ready, 1)
            keep_clock_up(WARM_UP)
            pe.wait_ge(const_ready, 1)
            pe.wait_ge(wq_loaded, 16)
            for half in range(2):
                for i in range(4):
                    mm = turn_weights(wq, pc[:, half], D, 4 * half + i, i)
                mm.then_inc(w_full, 1)
            pe.wait_ge(wk_loaded, 16)
            for half in range(2):
                for i in range(4):
                    mm = turn_weights(wk, pc[:, 2 + half], DC, 4 * half + i, i)
                mm.then_inc(w_full, 1)
            turn_x(0).then_inc(xnT_full, 1)
            for k in (0, 1):
                transpose_c(pro, k, k)
            pe.wait_ge(w_act, 2)
            pe.wait_ge(w_dve, 2)
            for h in range(H):
                product_g(h)
                if h == HG - 1:
                    transpose_c(pro, 2, 2)
            pe.wait_ge(xnT_lo_done, 1)
            pe.wait_ge(G_lo_done, 2)
            make_g(pro, 3, 0)
            pe.wait_ge(wv_loaded, 16)
            for half, bank in enumerate([pc[:, 0], scores[:, 0]]):
                for i in range(4):
                    mm = turn_weights(wv, bank, DC, 4 * half + i, i)
                mm.then_inc(w_full, 1)
            pe.wait_ge(G_lo_done, 4)
            make_g(pro, 4, 1)
            pe.wait_ge(ident16_ready, 1)
            for k, (what, m, _, _) in enumerate(PREP[5:], 5):
                WORK[what](pro, k, m)
                if (what, m) == ("max", 10):
                    for p in range(1, NP):
                        mm = turn_x(p)
                    mm.then_inc(xnT_full, 1)
                if what == "max" and 1 <= m < 1 + H:
                    if m == 1:
                        pe.wait_ge(wo_loaded, 16)
                    if m % HG == 1:
                        pe.wait_ge(w_act, 4 if m == 1 else 6)
                    product_m(m - 1)
                elif what == "max" and m > 0:
                    keep_clock_up(1 if m < NR * NC - 1 else 3)
            pe.wait_ge(late_const, 3)
            run_steps(pe, step)
            s = Step(B, TAIL)
            for j in range(NT - LAG, NT):
                p_times_c(s, j, -1)
            for k, (what, m, _, _) in enumerate(TAIL):
                WORK[what](s, k, m)

        @block.scalar
        def _(act):
            act.dma_start(wq[:, :], w_q).then_inc(wq_loaded, 16)
            act.dma_start(x_in[:, 1:NP], x_dram[:, 1:NP]).then_inc(x_rest_loaded, 16)
            act.dma_start(wo[:, :, :], w_out.rearrange("(b p) n -> p b n", p=128)).then_inc(wo_loaded, 16)
            act.dma_start(bias[:, :], b_out.rearrange("(a n) -> a n", a=1).to_broadcast([PAIR, D]))\
                .then_inc(bias_loaded, 16)

            def ct_hi(s, k, c):
                act.wait_ge(ct_full, s.times(NC, NC + c + 1))
                act.activation(cT_hi[0:DC, (s.t0 + 1) % 2, c * CW:(c + 1) * CW], side[0:DC, k % 2, 0:CW],
                               ACT.Copy).then_inc(ct_hi_done, 1)

            def g_hi_half(s, k, half):
                act.wait_ge(g_full, s.times(2, 2 + half + 1))
                act.activation(g_hi[:, (s.t0 + 1) % 2, half * HALF:(half + 1) * HALF],
                               side[0:DC, k % 2, 0:HALF], ACT.Copy, scale=G_DOWN).then_inc(g_hi_done, 1)

            def max_row(s, k, m):
                if m == 0:
                    act.wait_ge(mrow_full, s.times(2, 2 + m + 1))
                    act.activation(g_lo[DC:DC + 1, (s.t0 + 1) % 2, 0:512], side[DC:DC + 1, k % 2, 0:512],
                                   ACT.Copy).then_inc(side_free[k % 2], 1)

            def u_turned(s, k, m):
                act.wait_ge(ut_full, s.times(2, -2 + m + 1))
                e2, split = (s.t0 - 1) % 2, 512 // Q
                rest = 512 % Q
                if m == 0:
                    act.activation(uT[:, split, e2, 0:rest], side[0:DC, k % 2, split * Q:512], ACT.Copy)
                    heads, whole = slice(0, split), side[0:DC, k % 2, 0:split * Q]
                else:
                    act.activation(uT[:, split, e2, rest:Q], side[0:DC, k % 2, 0:Q - rest], ACT.Copy)
                    heads, whole = slice(split + 1, H), side[0:DC, k % 2, Q - rest:ROWS - 512]
                act.activation(uT[:, heads, e2, :], whole.rearrange("c (h q) -> c h q", q=Q),
                               ACT.Copy).then_inc(side_free[k % 2], 1)

            def rhs_out(s, k, m):
                if m == 1:
                    act.wait_ge(rhs_full, 2)
                    act.activation(rhs_i[:, :], side[:, k % 2, 0:D // 2].bitcast(F16), ACT.Copy)
                    act.activation(rhs_row[:, :], side[0:PAIR, k % 2, D:2 * D], ACT.Copy)\
                        .then_inc(side_free[k % 2], 1)

            WORK = {"ct": ct_hi, "g": g_hi_half, "mrow": max_row, "ut": u_turned, "rhs": rhs_out}

            def side_work(s, j, place):
                for k, what, m in at(s.schedule, j, place):
                    if what in WORK:
                        WORK[what](s, k, m)

            def exp_half(s, j, half):
                act.wait_ge(scores_full, s.times(2 * NT, 2 * j + half + 1))
                at_least(act, pc_done, s.times(NT, j - NPB + 1))
                act.activation(prob[:, j % NPB, half * HALF:(half + 1) * HALF], scores[0:KP, half, 0:HALF],
                               ACT.Exp).then_inc(exp_done, 1)

            def split_c(s):
                n2 = (s.t0 + 1) % 2
                at_least(act, c_loaded[n2], s.times(8, 24 if not n2 else 16))
                at_least(act, pc_done, s.times(NT))
                act.activation(cn[:, n2, :, 0:DC], c32[:, n2], ACT.Copy).then_inc(c_hi_done, 1)

            def step(s):
                for j in range(NT):
                    side_work(s, j, 0)
                    exp_half(s, j, 0)
                    side_work(s, j, 1)
                    exp_half(s, j, 1)
                    side_work(s, j, 2)
                    if j == 2 and s.t0 < B - 1:
                        split_c(s)

            def copy_weights(full, to, bank, rows):
                act.wait_ge(w_full, full)
                act.activation(to.rearrange("p a c -> p (a c)"), bank[:, 0:4 * rows], ACT.Copy).then_inc(w_act, 1)

            def copy_g(full, heads, bank):
                act.wait_ge(w_full, full)
                act.activation(G_hi[:, heads, :], bank[:, 0:4 * DC].rearrange("p (h c) -> p h c", h=4),
                               ACT.Copy, scale=G_UP).then_inc(G_hi_done, 1)

            def copy_xnT(full, bank, cols):
                act.wait_ge(xnT_full, full)
                act.activation(xnT_hi[:, cols], bank[:, cols], ACT.Copy).then_inc(xnT_hi_done, 1)

            pro = Prologue()
            copy_weights(1, wqT[:, 0:4, :], pc[:, 0], D)
            copy_weights(3, wkT[:, 0:4, :], pc[:, 2], DC)
            copy_xnT(1, scores[:, 0], slice(0, PAIR))
            ct_hi(pro, 0, 0)
            ct_hi(pro, 1, 1)
            for n, bank in enumerate(G_BANKS):
                copy_g(5 + n, EIGHT_HEADS[n], (scores[:, 1] if bank < 0 else pc[:, bank]))
                if n == 1:
                    ct_hi(pro, 2, 2)
            g_hi_half(pro, 3, 0)
            act.wait_ge(wvT_zeroed, 1)
            for half, bank in enumerate([pc[:, 0], scores[:, 0]]):
                act.wait_ge(w_full, 9 + half)
                for odd in (0, 1):
                    part = slice(DH * odd, DH * odd + DH)
                    act.activation(wvT[part, 8 * half + odd:8 * half + 8:2, :],
                                   bank[part, 0:4 * DC].rearrange("p (a c) -> p a c", a=4), ACT.Copy)\
                        .then_inc(w_act, 1)
                if half == 0:
                    g_hi_half(pro, 4, 1)
            split_c(pro)
            for n, bank in enumerate(M_BANKS):
                if n == 2:
                    copy_xnT(2, pc[:, 1], slice(PAIR, B * Q))
                    max_row(pro, use_of(PREP, "mrow", 0), 0)
                act.wait_ge(w_full, 11 + n)
                act.activation(M[:, 4 * n:4 * n + 4, :],
                               pc[0:DC, bank, 0:4 * D].rearrange("p (h c) -> p h c", h=4), ACT.Copy)\
                    .then_inc(w_act, 1)
            run_steps(act, step)
            s = Step(B, TAIL)
            for m in range(2):
                u_turned(s, m, m)

        @block.vector
        def _(dve):
            def ct_lo(s, k, c):
                n2 = (s.t0 + 1) % 2
                cols = slice(c * CW, (c + 1) * CW)
                dve.wait_ge(ct_hi_done, s.times(NC, NC + c + 1))
                dve.tensor_tensor(cT_lo[:, n2, cols], side[0:DC, k % 2, 0:CW], cT_hi[0:DC, n2, cols],
                                  ALU.subtract).then_inc(side_free[k % 2], 1)

            def g_lo_half(s, k, half):
                n2 = (s.t0 + 1) % 2
                cols = slice(half * HALF, (half + 1) * HALF)
                dve.wait_ge(g_hi_done, s.times(2, 2 + half + 1))
                dve.scalar_tensor_tensor(out=g_lo[0:DC, n2, cols], in0=side[0:DC, k % 2, 0:HALF],
                                         scalar=G_DOWN, in1=g_hi[:, n2, cols], op0=ALU.mult,
                                         op1=ALU.subtract).then_inc(side_free[k % 2], 1)

            def max_row(s, k, m):
                if m == 1:
                    dve.wait_ge(mrow_full, s.times(2, 2 + m + 1))
                    dve.tensor_copy(g_lo[DC:DC + 1, (s.t0 + 1) % 2, 512:ROWS],
                                    side[DC:DC + 1, k % 2, 0:ROWS - 512]).then_inc(side_free[k % 2], 1)

            def chunk_max(s, k, m):
                dve.wait_ge(max_full, s.times(NR * NC, NR * NC + m + 1))
                dve.tensor_reduce(maxes[:, m // NC, m % NC:m % NC + 1], side[:, k % 2, 0:CW], AX.X,
                                  ALU.max).then_inc(side_free[k % 2], 1)
                if m in MROW_AFTER:
                    dve.wait_ge(side_free[k % 2], s.freed(k + 2))
                    at_least(dve, mrow_full, s.times(2, 2))
                    tiles = slice(0, 4) if m == MROW_AFTER[0] else slice(4, NR)
                    dve.tensor_reduce(neg_max[:, tiles], maxes[:, tiles, :], AX.X, ALU.max,
                                      negate=True).then_inc(neg_max_done, 1)

            def take_u(s):
                dve.wait_ge(pc_done, s.times(NT))
                parts = [(slice(0, 4), pc[:, 0:4, 0:CN]), (slice(4, NR), pc[:, 0:NR - 4, CN:2 * CN])]
                for rows, acc in parts:
                    dve.reciprocal(rsum[:, rows], acc[:, :, DC]).then_inc(rsum_done, 1)
                for n, (rows, acc) in enumerate(parts):
                    dve.wait_ge(rsum_done, s.times(2, -2 + n + 1))
                    count = rows.stop - rows.start
                    dve.tensor_tensor(u_part[:, rows, :], acc,
                                      rsum[:, rows].rearrange("p (r a) -> p r a", a=1).to_broadcast([128, count, CN]),
                                      ALU.mult).then_inc(u_part_done, 1)

            def finish_x1(s, k, m):
                dve.wait_ge(out_full, s.pairs(2, m + 1))
                if m == 0:
                    if s.i is None:
                        resid = xb[:, s.pairs(1), :]
                    else:
                        resid = xb[:, bass.ds(s.pairs(1), 1), :].rearrange("p a d -> p (a d)")
                    dve.tensor_tensor(x1_part[:, :], side[0:PAIR, k % 2, 0:D], resid, ALU.add)\
                        .then_inc(side_free[k % 2], 1)
                    return
                k0 = [kk for kk, use in enumerate(s.schedule) if use[0] == "out"][0]
                dve.wait_ge(side_free[k0 % 2], s.freed(k0 + 2))
                dve.tensor_tensor(x1[:, :], side[0:PAIR, k % 2, 0:D], x1_part[:, :], ALU.add)\
                    .then_inc(side_free[k % 2], 1)
                dve.wait_ge(side_free[k % 2], s.freed(k + 2))
                dve.bn_stats(st2[:, :], x1[:, :]).then_inc(ffn_step, 1)

            def row_moments(s):
                dve.bn_aggr(mv2[:, :], st2[:, :]).then_inc(ffn_step, 1)
                dve.wait_ge(ffn_step, s.pairs(NFFN, 2))
                dve.tensor_scalar(ve2[:, :], mv2[:, 1:2], EPS, None, ALU.add).then_inc(ffn_step, 1)

            def normalise(s):
                dve.wait_ge(rstd2_done, s.pairs(1, 1))
                dve.tensor_scalar(xn2[:, :], x1[:, :], mv2[:, 0:1], rstd2[:, :], ALU.subtract, ALU.mult)\
                    .then_inc(ffn_step, 1)

            def row_max(s):
                dve.wait_ge(ffn_step, s.pairs(NFFN, 4))
                dve.tensor_reduce(row_sc[:, 0:1], xn2[:, :], AX.X, ALU.max, apply_absolute_value=True)\
                    .then_inc(ffn_step, 1)

            def row_scale(s):
                dve.wait_ge(ffn_step, s.pairs(NFFN, 5))
                dve.tensor_scalar(row_sc[:, 1:2], row_sc[:, 0:1], 1e-12, 1.0 / QMAX, ALU.max, ALU.mult)\
                    .then_inc(ffn_step, 1)

            def row_inverse(s):
                dve.wait_ge(ffn_step, s.pairs(NFFN, 6))
                dve.reciprocal(row_sc[:, 2:3], row_sc[:, 1:2]).then_inc(ffn_step, 1)

            def clip_high(s):
                dve.wait_ge(ffn_step, s.pairs(NFFN, 7))
                dve.tensor_scalar(q_a[:, :], xn2[:, :], row_sc[:, 2:3], QMAX, ALU.mult, ALU.min)\
                    .then_inc(ffn_step, 1)

            def clip_low(s):
                dve.wait_ge(ffn_step, s.pairs(NFFN, 8))
                dve.tensor_scalar(q_b[:, :], q_a[:, :], -QMAX, ROUND, ALU.max, ALU.add).then_inc(ffn_step, 1)

            def to_integers(s):
                dve.wait_ge(ffn_step, s.pairs(NFFN, 9))
                dve.tensor_scalar(q_i[:, :], q_b[:, :], ROUND, None, ALU.subtract).then_inc(ffn_step, 1)

            QUANTISE = {(8, 0): normalise, (8, 1): row_max, (8, 2): row_scale, (9, 0): row_inverse,
                        (9, 1): clip_high, (9, 2): clip_low, (10, 0): to_integers}

            def take_qT(s, k, m):
                dve.wait_ge(ft_full, s.pairs(1, 1))
                dve.tensor_copy(q_iT[:, :], side[:, k % 2, 0:PAIR // 2].bitcast(F16))\
                    .then_inc(side_free[k % 2], 1)

            def finish_pair(s, k, m):
                dve.wait_ge(fm_full, s.pairs(1, 1))
                dve.scalar_tensor_tensor(out=y_a[:, :], in0=side[0:PAIR, k % 2, 0:D], scalar=row_sc[:, 1:2],
                                         in1=rhs_row[:, :], op0=ALU.mult, op1=ALU.mult)\
                    .then_inc(side_free[k % 2], 1)
                dve.wait_ge(side_free[k % 2], s.freed(k + 2))
                if s.i is None:
                    y_pair = y[:, s.pairs(1), :]
                else:
                    y_pair = y[:, bass.ds(s.pairs(1), 1), :].rearrange("p a d -> p (a d)")
                dve.tensor_tensor(y_pair, y_a[:, :], x1[:, :], ALU.add).then_inc(y_done, 1)

            def rhs_quantise(s, k, m):
                if m != 0:
                    return
                dve.wait_ge(rhs_full, 1)
                rt = side[:, k % 2, 0:D]
                dve.tensor_reduce(rhs_sc[:, 0:1], rt, AX.X, ALU.max, apply_absolute_value=True)\
                    .then_inc(rhs_step, 1)
                dve.wait_ge(rhs_step, 1)
                dve.tensor_scalar(rhs_sc[:, 1:2], rhs_sc[:, 0:1], 1e-12, 1.0 / QMAX, ALU.max, ALU.mult)\
                    .then_inc(rhs_step, 1)
                dve.wait_ge(rhs_step, 2)
                dve.reciprocal(rhs_sc[:, 2:3], rhs_sc[:, 1:2]).then_inc(rhs_step, 1)
                dve.wait_ge(rhs_step, 3)
                dve.tensor_scalar(rhs_diag[:, :], rt, rhs_sc[:, 2:3], QMAX, ALU.mult, ALU.min)\
                    .then_inc(side_free[k % 2], 1)
                dve.wait_ge(side_free[k % 2], s.freed(k + 2))
                dve.tensor_scalar(rhsT_q[:, :], rhs_diag[:, :], -QMAX, ROUND, ALU.max, ALU.add)\
                    .then_inc(rhs_step, 1)
                dve.wait_ge(rhs_step, 4)
                dve.tensor_scalar(rhsT_i[:, :], rhsT_q[:, :], ROUND, None, ALU.subtract).then_inc(rhs_step, 1)
                dve.tensor_scalar(rhs_diag[:, :], ident[:, :], rhs_sc[:, 1:2], None, ALU.mult)\
                    .then_inc(rhs_step, 1)

            WORK = {"ct": ct_lo, "g": g_lo_half, "max": chunk_max, "mrow": max_row, "out": finish_x1, "ft": take_qT,
                    "fm": finish_pair, "rhs": rhs_quantise}

            def side_work(s, j, place):
                for k, what, m in at(s.schedule, j, place):
                    if what in WORK:
                        WORK[what](s, k, m)

            def prob_low(s, j, half):
                dve.wait_ge(exp_done, s.times(2 * NT, 2 * j + half + 1))
                cols = slice(half * HALF, (half + 1) * HALF)
                dve.tensor_tensor(prob_lo[:, j % NPB, cols], prob[:, j % NPB, cols], prob_hi[:, j % NPB, cols],
                                  ALU.subtract).then_inc(lo_dve, 1)

            def step(s):
                for j in range(NT):
                    if j == 2 and s.t0 > 0:
                        take_u(s)
                    pair = s.t0 > 0 and not s.odd
                    side_work(s, j, 0)
                    if pair and (j, 0) in QUANTISE:
                        QUANTISE[j, 0](s)
                    side_work(s, j, 1)
                    if pair and (j, 1) in QUANTISE:
                        QUANTISE[j, 1](s)
                    moments = j == 6 and pair
                    if moments:
                        dve.wait_ge(ffn_step, s.pairs(NFFN, 1))
                    for jh in low_parts(s.t0)[0]:
                        if jh[0] == j:
                            prob_low(s, *jh)
                    if moments:
                        row_moments(s)
                    side_work(s, j, 2)
                    if pair and (j, 2) in QUANTISE:
                        QUANTISE[j, 2](s)

            dve.memset(ones[:, :], 1.0).then_inc(ones_ready, 1)
            dve.memset(minus_half[:, :], -0.5).then_inc(minus_half_ready, 1)
            dve.memset(cn[:, :, :, DC:DC + 1], 1.0).then_inc(late_const, 1)
            dve.memset(cT_hi[DC:DC + 1, 0, :], 1.0).then_inc(late_const, 1)

            def ln_moments(pairs, counted):
                for n, p in enumerate(pairs):
                    dve.bn_stats(st1[:, p, :], x_in[:, p, :]).then_inc(ln_step, 1)
                for n, p in enumerate(pairs):
                    dve.wait_ge(ln_step, counted + n + 1)
                    dve.bn_aggr(mv1[:, p, :], st1[:, p, :]).then_inc(ln_step, 1)
                dve.wait_ge(ln_step, counted + 2 * len(pairs))
                dve.tensor_scalar(ve1[:, pairs[0]:pairs[-1] + 1], mv1[:, pairs[0]:pairs[-1] + 1, 1], EPS, None,
                                  ALU.add).then_inc(ln_step, 1)

            def ln_apply(p):
                dve.tensor_scalar(xn[:, p, :], x_in[:, p, :], mv1[:, p, 0:1], rstd1[:, p:p + 1],
                                  ALU.subtract, ALU.mult).then_inc(xn_done, 1)

            def copy_weights(full, to, bank, rows):
                dve.wait_ge(w_full, full)
                dve.tensor_copy(to.rearrange("p a c -> p (a c)"), bank[:, 0:4 * rows]).then_inc(w_dve, 1)

            def low_g(n):
                heads, bank = EIGHT_HEADS[n], (scores[:, 1] if G_BANKS[n] < 0 else pc[:, G_BANKS[n]])
                dve.wait_ge(G_hi_done, n + 1)
                dve.scalar_tensor_tensor(out=G_lo[:, heads, :],
                                         in0=bank[:, 0:4 * DC].rearrange("p (h c) -> p h c", h=4),
                                         scalar=G_UP, in1=G_hi[:, heads, :], op0=ALU.mult, op1=ALU.subtract)\
                    .then_inc(G_lo_done, 1)

            def low_xnT(hi_done, bank, cols):
                dve.wait_ge(xnT_hi_done, hi_done)
                dve.tensor_tensor(xnT_lo[:, cols], bank[:, cols], xnT_hi[:, cols], ALU.subtract)\
                    .then_inc(xnT_lo_done, 1)

            dve.wait_ge(x_loaded, 16)
            ln_moments([0], 0)
            dve.wait_ge(ln_rstd, 1)
            ln_apply(0)
            copy_weights(2, wqT[:, 4:8, :], pc[:, 1], D)
            copy_weights(4, wkT[:, 4:8, :], pc[:, 3], DC)
            pro = Prologue()
            low_xnT(1, scores[:, 0], slice(0, PAIR))
            ct_lo(pro, 0, 0)
            dve.wait_ge(x_rest_loaded, 16)
            ln_moments([1, 2, 3], 3)
            ct_lo(pro, 1, 1)
            for n in range(4):
                low_g(n)
                if n == 1:
                    ct_lo(pro, 2, 2)
            g_lo_half(pro, 3, 0)
            chunk_max(pro, 5, 0)
            g_lo_half(pro, 4, 1)
            dve.wait_ge(ln_rstd, 2)
            for k, (what, m, _, _) in enumerate(PREP[6:], 6):
                WORK[what](pro, k, m)
                if what == "max" and 4 <= m < 4 + NP - 1:
                    ln_apply(m - 3)
            low_xnT(2, pc[:, 1], slice(PAIR, B * Q))
            dve.wait_ge(xb_ready, 1)
            run_steps(dve, step)
            s = Step(B, TAIL)
            take_u(s)
            dve.wait_ge(u_part_done, s.times(2))
            dve.tensor_tensor(u[:, :, :], u_part[:, :, 0:DC], u_part[:, :, DC + 1:CN], ALU.add).then_inc(u_done, 1)
            for k, (what, m, _, _) in enumerate(TAIL):
                if what in WORK:
                    WORK[what](s, k, m)
                if (what, m) == ("out", 1):
                    dve.wait_ge(ffn_step, s.pairs(NFFN, 1))
                    row_moments(s)
                    for operation in QUANTISE.values():
                        operation(s)

        @block.gpsimd
        def _(pool):
            def prob_low(s, j, half):
                pool.wait_ge(exp_done, s.times(2 * NT, 2 * j + half + 1))
                cols = slice(half * HALF, (half + 1) * HALF)
                pool.tensor_tensor(prob_lo[:, j % NPB, cols], prob[:, j % NPB, cols], prob_hi[:, j % NPB, cols],
                                   ALU.subtract).then_inc(lo_pool, 1)

            def add_u(s):
                pool.wait_ge(u_part_done, s.times(2))
                at_least(pool, ut_full, s.times(2, -2))
                pool.tensor_tensor(u[:, :, :], u_part[:, :, 0:DC], u_part[:, :, DC + 1:CN],
                                   ALU.add).then_inc(u_done, 1)

            def split_c(s):
                n2 = (s.t0 + 1) % 2
                pool.wait_ge(c_hi_done, s.times(1, 2))
                pool.tensor_tensor(cn[:, n2, :, DC + 1:CN], c32[:, n2], cn[:, n2, :, 0:DC],
                                   ALU.subtract).then_inc(c_lo_done, 1)

            def row_std(s):
                pool.wait_ge(ffn_step, s.pairs(NFFN, 3))
                pool.tensor_tensor(rstd2[:, :], ve2[:, :], minus_half[0:PAIR, 0:1], ALU.pow)\
                    .then_inc(rstd2_done, 1)

            def step(s):
                for j in range(NT):
                    if j == 3 and s.t0 > 0:
                        add_u(s)
                    if j == 4 and s.t0 < B - 1:
                        split_c(s)
                    if j == 7 and s.t0 > 0 and not s.odd:
                        row_std(s)
                    for jh in low_parts(s.t0)[1]:
                        if jh[0] == j:
                            prob_low(s, *jh)

            pool.memset(ident[:, :], 0.0).then_inc(const_step, 1)
            pool.wait_ge(const_step, 1)
            pool.affine_select(out=ident[:, :], in_=ident[:, :], compare_op=ALU.not_equal, fill=1.0, base=0,
                               pattern=[[-1, 128]], channel_multiplier=1).then_inc(const_ready, 1)
            pool.wait_ge(minus_half_ready, 1)
            pool.wait_ge(ln_step, 3)
            pool.tensor_tensor(rstd1[:, 0:1], ve1[:, 0:1], minus_half[0:PAIR, 0:1], ALU.pow).then_inc(ln_rstd, 1)
            pool.memset(wvT[:, :, :], 0.0).then_inc(wvT_zeroed, 1)
            pool.wait_ge(ln_step, 2 * NP + 2)
            pool.tensor_tensor(rstd1[:, 1:NP], ve1[:, 1:NP], minus_half[0:PAIR, 1:NP], ALU.pow)\
                .then_inc(ln_rstd, 1)
            pool.wait_ge(const_ready, 1)
            pool.tensor_copy(ident16[:, :], ident[:, :]).then_inc(ident16_ready, 1)
            split_c(Prologue())
            pool.wait_ge(bias_loaded, 16)
            pool.wait_ge(x_rest_loaded, 16)
            pool.tensor_tensor(xb[:, :, :], x_in[:, :, :],
                               bias[:, :].rearrange("p (a d) -> p a d", a=1).to_broadcast([PAIR, NP, D]),
                               ALU.add).then_inc(xb_ready, 1)
            pool.wait_ge(xb_ready, 1)
            pool.memset(cT_hi[DC:DC + 1, 1, :], 1.0).then_inc(late_const, 1)
            pool.wait_ge(late_const, 3)
            run_steps(pool, step)
            row_std(Step(B, TAIL))


_INS = ["x", "ctx_768", "L0_xattn_w_q", "L0_xattn_w_k", "L0_xattn_w_v", "L0_xattn_w_out", "L0_xattn_b_out",
        "L0_ffn_rhs"]


def kernel(**inputs):
    import numpy as _np
    import concourse.bacc as _bacc
    from concourse import mybir as _mybir
    from concourse.bass_utils import run_bass_kernel_spmd as _run

    nc = _bacc.Bacc("TRN2", target_bir_lowering=False, num_devices=1)
    arrays, args = {}, []
    for name in _INS:
        a = _np.ascontiguousarray(inputs[name])
        arrays[f"in_{name}"] = a
        args.append(nc.dram_tensor(f"in_{name}", a.shape, _mybir.dt.from_np(a.dtype), kind="ExternalInput").ap())
    args.append(nc.dram_tensor("out_y", (B, Q, D), F32, kind="ExternalOutput").ap())
    build(nc, *args)
    r = _run(nc, [arrays], core_ids=[0])
    return r.results[0]["out_y"]
```

```python
from contextlib import ExitStack

import concourse.bass as bass
from concourse import mybir

F32 = mybir.dt.float32
F16 = mybir.dt.float16
BF16 = mybir.dt.bfloat16
ALU = mybir.AluOpType
ACT = mybir.ActivationFunctionType
AX = mybir.AxisListType

B, Q, D = 8, 56, 128
KV, DC = 1500, 96
H, DH = 16, 64
KP = 125
NT = KV // KP
ROWS = H * Q
HALF = ROWS // 2
NR = ROWS // 128
NC = 3
TC = NT // NC
CW = KV // NC
CN = 2 * DC + 1
PAIR = 2 * Q
NP = B // 2
REST = (B - 2) * Q
HG = H // 2
LAG = 2
NPB = 4
G_UP = 16.0
G_DOWN = DH ** -0.5 / G_UP
M_UP = 16.0
EPS = 1e-5
QMAX = 127.0
ROUND = 1.5 * 2.0 ** 23
WARM_UP = 10
TAIL_WARM = {("ut", 0): 10, ("ut", 1): 5, ("ft", 0): 16}
NFFN = 10

TILES = [(j, h) for j in range(NT) for h in (0, 1)]
LO_DVE = [(j, 0) for j in range(NT) if j not in (0, 2, 7, 10)]
LO_DVE_LAST = [(j, h) for j, h in TILES if h == 0 or j % 2 == 1]

CT = [(0, 0, "ct", 0), (0, 1, "ct", 1), (1, 0, "ct", 2)]
G = [(1, 1, "g", 0), (2, 0, "g", 1)]
M_LATE = [(2, 1, "m", 2), (11, 2, "m", 3)]
UT = [(4, 0, "ut", 0), (5, 0, "ut", 1)]
RHS = [(4, 0, "rhs", 0), (6, 0, "rhs", 1)]
OUT = [(5, 1, "out", 0), (6, 0, "out", 1), (11, 0, "ft", 0), (11, 2, "fm", 0)]
MAX_AT = [(3, 0), (3, 1), (3, 2), (4, 2), (5, 1), (5, 2), (6, 0), (6, 1), (6, 2), (7, 0), (7, 1),
          (7, 2), (8, 0), (8, 1), (8, 2), (9, 0), (9, 1), (9, 2), (10, 0), (10, 1), (10, 2)]
MAXES = [(j, a, "max", m) for m, (j, a) in enumerate(MAX_AT)]
MROW = [(9, 0, "mrow", 0), (11, 1, "mrow", 1)]
MROW_AFTER = [3 * NC + 2, NR * NC - 1]


EIGHT_HEADS = [slice(0, 8, 2), slice(1, 8, 2), slice(8, H, 2), slice(9, H, 2)]
G_BANKS = [-1, 2, 3, 1]
M_AT = {16: [0], 17: [1], 18: [2], 19: [3], 20: [4, 5, 6, 7]}
GREST_BANKS = [1, 2, 3]
POOL_REST_LATER = 6


def in_order(*lists):
    return [(what, m, j, a) for j, a, _, what, m in
            sorted((j, a, n, what, m) for n, l in enumerate(lists) for j, a, what, m in l)]


def prepare():
    yield from (("ct", 0), ("ct", 1), ("ct", 2), ("g", 0), ("g", 1))
    for m in range(NR * NC):
        yield "max", m
        if m == MROW_AFTER[0] + 2:
            yield "mrow", 0
    yield "mrow", 1


PREP = [(what, m, 0, 0) for what, m in prepare()]
FIRST = in_order(RHS, CT, G, M_LATE, MAXES, MROW)
ODD = in_order(UT, CT, MAXES, MROW)
EVEN = in_order(OUT, UT, CT, MAXES, MROW)
LAST = in_order(UT)
TAIL = [("ut", 0, 0, 0), ("ut", 1, 0, 0), ("out", 0, 0, 0), ("out", 1, 0, 0), ("ft", 0, 0, 0), ("fm", 0, 0, 0)]
assert all(len(s) % 2 == 0 for s in (PREP, FIRST, ODD, EVEN, LAST, TAIL))


def uses(schedule, bank):
    return (len(schedule) + 1 - bank) // 2


class Step:

    def __init__(self, t0, schedule, i=None):
        self.t0, self.i, self.schedule = t0, i, schedule
        self.odd = t0 % 2

    def times(self, per, more=0):
        fixed = per * self.t0 + more
        return fixed if self.i is None else self.i * (2 * per) + fixed

    def pairs(self, per, more=0):
        fixed = per * ((self.t0 - 1) // 2) + more
        return fixed if self.i is None else self.i * per + fixed

    def freed(self, k):
        bank = k % 2
        fixed = uses(PREP, bank) + k // 2
        if self.t0 > 0:
            fixed += uses(FIRST, bank)
        if self.i is not None:
            if not self.odd:
                fixed += uses(ODD, bank)
            return self.i * (uses(ODD, bank) + uses(EVEN, bank)) + fixed
        if self.t0 > 0:
            fixed += 3 * (uses(ODD, bank) + uses(EVEN, bank))
        if self.t0 > B - 1:
            fixed += uses(LAST, bank)
        return fixed


class Prologue(Step):

    def __init__(self):
        super().__init__(-1, PREP)
        self.odd = 1

    def freed(self, k):
        return k // 2


def rows_of(s, dt, start, width):
    first = s.times(ROWS, dt * ROWS + start)
    return slice(first, first + width) if s.i is None else bass.ds(first, width)


def low_parts(batch):
    by_dve = LO_DVE_LAST if batch == B - 1 else LO_DVE
    return by_dve, [jh for jh in TILES if jh not in by_dve]


def at_least(eng, sem, value):
    if not isinstance(value, int) or value > 0:
        eng.wait_ge(sem, value)


def run_steps(eng, step):
    step(Step(0, FIRST))
    with eng.Fori(0, (B - 2) // 2) as i:
        step(Step(1, ODD, i))
        step(Step(2, EVEN, i))
    step(Step(B - 1, LAST))


def use_of(schedule, what, m):
    return [k for k, use in enumerate(schedule) if use[:2] == (what, m)][0]


def at(schedule, j, place):
    return [(k, what, m) for k, (what, m, jj, a) in enumerate(schedule) if (jj, a) == (j, place)]


def build(nc, x, ctx_kv, w_q, w_k, w_v, w_out, b_out, rhs, out):
    with ExitStack() as stack:
        def sb(name, shape, dt):
            return stack.enter_context(nc.sbuf_tensor(name, shape, dt))

        def psum(name, shape, dt):
            return stack.enter_context(nc.psum_tensor(name, shape, dt))

        def sem(name):
            return stack.enter_context(nc.semaphore(name))

        scores = psum("scores", [128, 2, 512], F32)
        side = psum("side", [128, 2, 512], F32)
        pc = psum("pc", [128, 4, 512], F32)

        ident = sb("ident", [128, 128], F32)
        ident16 = sb("ident16", [128, 128], F16)
        ones = sb("ones", [128, PAIR], F32)
        minus_half = sb("minus_half", [128, NP], F32)
        wq = sb("wq", [D, H * DH], F32)
        wk = sb("wk", [DC, H * DH], F32)
        wv = sb("wv", [DC, H * DH], F32)
        wo = sb("wo", [128, H // 2, D], F32)
        wqT = sb("wqT", [128, H // 2, D], F32)
        wkT = sb("wkT", [128, H // 2, DC], F32)
        wvT = sb("wvT", [128, H, DC], F32)
        G_hi = sb("G_hi", [D, H, DC], F16)
        G_lo = sb("G_lo", [D, H, DC], F16)
        M_hi = sb("M_hi", [DC, H, D], F16)
        M_lo = sb("M_lo", [DC, H, D], F16)
        bias = sb("bias", [PAIR, D], F32)
        rhs_in = sb("rhs_in", [D, D], F32)
        rhsT_q = sb("rhsT_q", [D, D], F32)
        rhsT_i = sb("rhsT_i", [D, D], F16)
        rhs_i = sb("rhs_i", [D, D], F16)
        rhs_sc = sb("rhs_sc", [D, 4], F32)
        rhs_diag = sb("rhs_diag", [D, D], F32)
        rhs_row = sb("rhs_row", [PAIR, D], F32)

        x_in = sb("x_in", [PAIR, NP, D], F32)
        xn = sb("xn", [PAIR, NP, D], F32)
        xb = sb("xb", [PAIR, NP, D], F32)
        xnT_hi = sb("xnT_hi", [D, B * Q], F16)
        xnT_lo = sb("xnT_lo", [D, B * Q], F16)
        st1 = sb("st1", [PAIR, NP, 6], F32)
        mv1 = sb("mv1", [PAIR, NP, 2], F32)
        ve1 = sb("ve1", [PAIR, NP], F32)
        rstd1 = sb("rstd1", [PAIR, NP], F32)

        g_hi = sb("g_hi", [DC, B * ROWS], F16)
        g_lo = sb("g_lo", [DC + 1, B * ROWS], F16)
        g32 = sb("g32", [DC, H, REST], F32)

        c32 = sb("c32", [KP, 2, NT, DC], F32)
        cn = sb("cn", [KP, 2, NT, CN + 1], F16)
        cT_hi = sb("cT_hi", [DC + 1, 2, KV], F16)
        cT_lo = sb("cT_lo", [DC, 2, KV], F16)
        maxes = sb("maxes", [128, NR, NC], F32)
        neg_max = sb("neg_max", [128, NR], F16)
        prob = sb("prob", [KP, NPB, ROWS], F32)
        prob_lo = sb("prob_lo", [KP, NPB, ROWS], F16)
        rsum = sb("rsum", [128, NR], F32)
        u_part = sb("u_part", [128, NR, CN], F32)
        u = sb("u", [128, NR, DC], F32)
        uT_hi = sb("uT_hi", [DC, H, 2, Q], F16)
        uT_lo = sb("uT_lo", [DC, H, 2, Q], F16)

        x1_part = sb("x1_part", [PAIR, D], F32)
        x1 = sb("x1", [PAIR, D], F32)
        st2 = sb("st2", [PAIR, 6], F32)
        mv2 = sb("mv2", [PAIR, 2], F32)
        ve2 = sb("ve2", [PAIR, 1], F32)
        rstd2 = sb("rstd2", [PAIR, 1], F32)
        xn2 = sb("xn2", [PAIR, D], F32)
        row_sc = sb("row_sc", [PAIR, 3], F32)
        q_a = sb("q_a", [PAIR, D], F32)
        q_b = sb("q_b", [PAIR, D], F32)
        q_i = sb("q_i", [PAIR, D], F16)
        q_iT = sb("q_iT", [D, PAIR], F16)
        y_a = sb("y_a", [PAIR, D], F32)
        y = sb("y", [PAIR, NP, D], F32)

        prob_hi = prob[:, :, :].bitcast(BF16).rearrange("p b (n two) -> p b n two", two=2)[:, :, :, 1]

        x_loaded, x_rest_loaded = sem("x_loaded"), sem("x_rest_loaded")
        wq_loaded, wk_loaded = sem("wq_loaded"), sem("wk_loaded")
        wv_loaded, wo_loaded, rhs_loaded = sem("wv_loaded"), sem("wo_loaded"), sem("rhs_loaded")
        bias_loaded = sem("bias_loaded")
        c_loaded = [sem("c_loaded_even"), sem("c_loaded_odd")]
        out_stored = sem("out_stored")
        wvT_zeroed, ident16_ready = sem("wvT_zeroed"), sem("ident16_ready")
        ones_ready = sem("ones_ready")
        const_ready = sem("const_ready")
        w_full = sem("w_full")
        w_act, w_dve = sem("w_act"), sem("w_dve")
        G_hi_done, G_lo_done = sem("G_hi_done"), sem("G_lo_done")
        ln_step, ln_rstd, xn_done = sem("ln_step"), sem("ln_rstd"), sem("xn_done")
        xnT_full, xnT_hi_done, xnT_lo_done = sem("xnT_full"), sem("xnT_hi_done"), sem("xnT_lo_done")
        rhs_step = sem("rhs_step")
        const_step = sem("const_step")
        late_const = sem("late_const")
        minus_half_ready, xb_ready = sem("minus_half_ready"), sem("xb_ready")
        scores_full = sem("scores_full")
        pc_done = sem("pc_done")
        ct_full, g_full = sem("ct_full"), sem("g_full")
        grest_full, grest_copied, grest_lo_done = sem("grest_full"), sem("grest_copied"), sem("grest_lo_done")
        m_full = sem("m_full")
        M_hi_done, M_lo_done = sem("M_hi_done"), sem("M_lo_done")
        max_full, mrow_full = sem("max_full"), sem("mrow_full")
        ut_full = sem("ut_full")
        out_full, ft_full, fm_full = sem("out_full"), sem("ft_full"), sem("fm_full")
        rhs_full = sem("rhs_full")
        side_free = [sem("side0_free"), sem("side1_free")]
        exp_done = sem("exp_done")
        ct_hi_done, g_hi_done = sem("ct_hi_done"), sem("g_hi_done")
        c_hi_done = sem("c_hi_done")
        ut_hi_done = sem("ut_hi_done")
        lo_pool = sem("lo_pool")
        c_lo_done = sem("c_lo_done")
        u_done = sem("u_done")
        rstd2_done = sem("rstd2_done")
        lo_dve = sem("lo_dve")
        neg_max_done = sem("neg_max_done")
        rsum_done, u_part_done = sem("rsum_done"), sem("u_part_done")
        ffn_step = sem("ffn_step")
        y_done = sem("y_done")

        def g_rest(g, head):
            return g.rearrange("c (b r) -> c b r", r=ROWS)[:, 2:B, head * Q:(head + 1) * Q]

        def turned_u(s, m):
            e2, split = (s.t0 - 1) % 2, 512 // Q
            rest = 512 % Q
            if m == 0:
                return [(lambda t: t[:, split, e2, 0:rest], lambda b: b[:, split * Q:512]),
                        (lambda t: t[:, 0:split, e2, :],
                         lambda b: b[:, 0:split * Q].rearrange("c (h q) -> c h q", q=Q))]
            return [(lambda t: t[:, split, e2, rest:Q], lambda b: b[:, 0:Q - rest]),
                    (lambda t: t[:, split + 1:H, e2, :],
                     lambda b: b[:, Q - rest:ROWS - 512].rearrange("c (h q) -> c h q", q=Q))]

        def add_parts(eng, s, n):
            eng.wait_ge(u_part_done, s.times(2, -1 + n))
            at_least(eng, ut_full, s.times(2, -2))
            rows = slice(0, 4) if n == 0 else slice(4, NR)
            eng.tensor_tensor(u[:, rows, :], u_part[:, rows, 0:DC], u_part[:, rows, DC + 1:CN],
                              ALU.add).then_inc(u_done, 1)

        block = stack.enter_context(nc.Block())

        c_dram = ctx_kv.rearrange("b (p j) d -> b p j d", j=NT)
        x_dram = x.rearrange("(n two) q d -> (two q) n d", two=2)
        out_dram = out.rearrange("(n two) q d -> n (two q) d", two=2)

        @block.sync
        def _(sp):
            sp.dma_start(x_in[:, 0], x_dram[:, 0]).then_inc(x_loaded, 16)
            sp.dma_start(x_in[:, 1:NP], x_dram[:, 1:NP]).then_inc(x_rest_loaded, 16)
            sp.dma_start(c32[:, 0], c_dram[0]).then_inc(c_loaded[0], 16)
            sp.dma_start(wv[:, :], w_v).then_inc(wv_loaded, 16)
            sp.dma_start(c32[:, 1], c_dram[1]).then_inc(c_loaded[1], 16)
            sp.dma_start(rhs_in[:, :], rhs).then_inc(rhs_loaded, 16)
            for b in range(2, B):
                sp.wait_ge(ct_full, NC * (b - 1))
                sp.wait_ge(c_lo_done, b - 1)
                sp.dma_start(c32[:, b % 2], c_dram[b]).then_inc(c_loaded[b % 2], 16)
                if b >= 5 and b % 2 == 1:
                    p = (b - 5) // 2
                    sp.wait_ge(y_done, p + 1)
                    sp.dma_start(out_dram[p], y[:, p, :]).then_inc(out_stored, 16)
            for p in range(2, NP):
                sp.wait_ge(y_done, p + 1)
                sp.dma_start(out_dram[p], y[:, p, :]).then_inc(out_stored, 16)
            sp.wait_ge(out_stored, 16 * NP)

        @block.tensor
        def _(pe):
            def side_bank(s, k):
                at_least(pe, side_free[k % 2], s.freed(k))
                return side[:, k % 2]

            def transpose_c(s, k, c):
                n2 = (s.t0 + 1) % 2
                if c == 0:
                    at_least(pe, c_loaded[n2], s.times(8, 24 if not n2 else 16))
                bank = side_bank(s, k)
                for jj in range(TC):
                    mm = pe.transpose(bank[0:DC, jj * KP:(jj + 1) * KP], c32[:, n2, c * TC + jj],
                                      ident[0:KP, 0:KP])
                mm.then_inc(ct_full, 1)

            def make_g(s, k, half):
                bank = side_bank(s, k)
                cols = slice((s.t0 + 1) * Q, (s.t0 + 2) * Q)
                for h in range(HG):
                    part, head = bank[0:DC, h * Q:(h + 1) * Q], half * HG + h
                    pe.matmul(part, G_hi[:, head, :], xnT_hi[:, cols], start=True, stop=False)
                    pe.matmul(part, G_hi[:, head, :], xnT_lo[:, cols], start=False, stop=False)
                    mm = pe.matmul(part, G_lo[:, head, :], xnT_hi[:, cols], start=False, stop=True)
                mm.then_inc(g_full, 1)

            def make_g_rest(head):
                if head >= len(GREST_BANKS):
                    pe.wait_ge(grest_copied, head - len(GREST_BANKS) + 1)
                part, cols = pc[0:DC, GREST_BANKS[head % 3], 0:REST], slice(B * Q - REST, B * Q)
                pe.matmul(part, G_hi[:, head, :], xnT_hi[:, cols], start=True, stop=False)
                pe.matmul(part, G_hi[:, head, :], xnT_lo[:, cols], start=False, stop=False)
                pe.matmul(part, G_lo[:, head, :], xnT_hi[:, cols], start=False, stop=True)\
                    .then_inc(grest_full, 1)

            def product_m(bank, h):
                return pe.matmul(bank[0:DC, h % 4 * D:(h % 4 + 1) * D], wvT[:, h, :], wo[:, h // 2, :], start=True,
                                 stop=True)

            def make_m(s, k, n):
                bank = side_bank(s, k)
                for h in range(4 * n, 4 * n + 4):
                    mm = product_m(bank, h)
                mm.then_inc(m_full, 1)

            def first_pass(s, k, m):
                n2 = (s.t0 + 1) % 2
                r, c = m // NC, m % NC
                if m == 0:
                    pe.wait_ge(ct_hi_done, s.times(NC, 2 * NC))
                    if s.t0 < 1:
                        pe.wait_ge(g_hi_done, s.times(2, 3))
                    else:
                        pe.wait_ge(grest_copied, H)
                if m == 3 * NC and s.t0 < 1:
                    pe.wait_ge(g_hi_done, s.times(2, 4))
                bank = side_bank(s, k)
                pe.matmul(bank[:, 0:CW], g_hi[:, rows_of(s, 1, r * 128, 128)],
                          cT_hi[0:DC, n2, c * CW:(c + 1) * CW], start=True, stop=True).then_inc(max_full, 1)

            def turn_max(s, k, m):
                bank = side_bank(s, k)
                pe.wait_ge(neg_max_done, s.times(2, 3 + m))
                for r in range(4 * m, min(4 * m + 4, NR)):
                    mm = pe.matmul(bank[DC:DC + 1, (r % 4) * 128:(r % 4 + 1) * 128], neg_max[:, r:r + 1],
                                   ident16[:, :], start=True, stop=True)
                mm.then_inc(mrow_full, 1)

            def turn_u(s, k, m):
                bank = side_bank(s, k)
                pe.wait_ge(u_done, s.times(2, -1 + m))
                for r in range(4 * m, min(4 * m + 4, NR)):
                    mm = pe.transpose(bank[0:DC, (r % 4) * 128:(r % 4 + 1) * 128], u[:, r, :], ident[:, :])
                mm.then_inc(ut_full, 1)

            def project_out(s, k, m):
                bank = side_bank(s, k)
                ku = use_of(s.schedule, "ut", m)
                pe.wait_ge(side_free[ku % 2], s.freed(ku + 2))
                for h in range(HG):
                    head = m * HG + h
                    hi = uT_hi[:, head].rearrange("c b q -> c (b q)")
                    lo = uT_lo[:, head].rearrange("c b q -> c (b q)")
                    pe.matmul(bank[0:PAIR, 0:D], hi, M_hi[:, head, :], start=(h == 0), stop=False)
                    pe.matmul(bank[0:PAIR, 0:D], hi, M_lo[:, head, :], start=False, stop=False)
                    mm = pe.matmul(bank[0:PAIR, 0:D], lo, M_hi[:, head, :], start=False, stop=(h == HG - 1))
                mm.then_inc(out_full, 1)

            def turn_q(s, k, m):
                bank = side_bank(s, k)
                pe.wait_ge(ffn_step, s.pairs(NFFN, NFFN))
                pe.transpose(bank[:, 0:PAIR // 2].bitcast(F16), q_i[:, :],
                             ident16[0:PAIR, 0:PAIR]).then_inc(ft_full, 1)

            def linear(s, k, m):
                bank = side_bank(s, k)
                kt = [kk for kk, use in enumerate(s.schedule) if use[0] == "ft"][0]
                pe.wait_ge(side_free[kt % 2], s.freed(kt + 2))
                pe.matmul(bank[0:PAIR, 0:D], q_iT[:, :], rhs_i[:, :], start=True, stop=True)\
                    .then_inc(fm_full, 1)

            def rhs_work(s, k, m):
                bank = side_bank(s, k)
                if m == 0:
                    pe.wait_ge(rhs_loaded, 16)
                    pe.transpose(bank[:, 0:D], rhs_in[:, :], ident[:, :]).then_inc(rhs_full, 1)
                else:
                    pe.wait_ge(rhs_step, 6)
                    pe.transpose(bank[:, 0:D // 2].bitcast(F16), rhsT_i[:, :], ident16[:, :])
                    pe.matmul(bank[0:PAIR, D:2 * D], ones[:, :], rhs_diag[:, :], start=True, stop=True)\
                        .then_inc(rhs_full, 1)

            WORK = {"ct": transpose_c, "g": make_g, "m": make_m, "max": first_pass, "mrow": turn_max, "ut": turn_u,
                    "out": project_out, "ft": turn_q, "fm": linear, "rhs": rhs_work}

            def side_work(s, j, place):
                for k, what, m in at(s.schedule, j, place):
                    WORK[what](s, k, m)

            def second_pass(s, j, half):
                b2 = s.t0 % 2
                kv = slice(j * KP, (j + 1) * KP)
                cols = rows_of(s, 0, half * HALF, HALF)
                if j == 0:
                    before = PREP if s.t0 == 0 else FIRST if s.t0 == 1 and s.i is None else \
                        ODD if s.t0 == 2 else EVEN
                    km = use_of(before, "mrow", half)
                    later = len(range(km + 2, len(before), 2))
                    pe.wait_ge(side_free[km % 2], s.freed(km % 2) - later)
                    if s.t0 >= 2:
                        pe.wait_ge(grest_lo_done, H)
                at_least(pe, exp_done, s.times(2 * NT, 2 * j + half - 1))
                bank = scores[0:KP, half, 0:HALF]
                pe.matmul(bank, cT_hi[:, b2, kv], g_lo[:, cols], start=True, stop=False)
                pe.matmul(bank, cT_lo[:, b2, kv], g_hi[:, cols], start=False, stop=False)
                pe.matmul(bank, cT_hi[0:DC, b2, kv], g_hi[:, cols], start=False, stop=True)\
                    .then_inc(scores_full, 1)

            def p_times_c(s, j, t0_off=0):
                b2 = (s.t0 + t0_off) % 2
                pe.wait_ge(exp_done, s.times(2 * NT, 2 * NT * t0_off + 2 * j + 2))
                for sem_lo, mine, usual in zip((lo_dve, lo_pool), low_parts(s.t0 + t0_off), low_parts(0)):
                    upto = sum(jj <= j for jj, _ in mine)
                    at_least(pe, sem_lo, s.times(len(usual), len(usual) * t0_off + upto))
                if j == 0 and s.t0 == 0:
                    pe.wait_ge(M_lo_done, 2)
                    pe.wait_ge(grest_copied, H)
                    pe.wait_ge(xnT_lo_done, 2)
                if j == 0:
                    pe.wait_ge(c_lo_done, s.times(1, 1 + t0_off))
                    at_least(pe, u_part_done, s.times(2, 2 * t0_off))
                for r in range(NR):
                    rows = slice(r * 128, (r + 1) * 128)
                    acc = pc[:, r % 4, (r // 4) * CN:(r // 4 + 1) * CN]
                    pe.matmul(acc, prob_hi[:, j % NPB, rows], cn[:, b2, j, 0:CN],
                              start=(j == 0 and r < 4), stop=False, skip_group_check=True)
                    mm = pe.matmul(acc[:, 0:DC + 1], prob_lo[:, j % NPB, rows], cn[:, b2, j, 0:DC + 1],
                                   start=False, stop=(j == NT - 1), skip_group_check=True)
                mm.then_inc(pc_done, 1)

            def step(s):
                for j in range(NT):
                    side_work(s, j, 0)
                    second_pass(s, j, 0)
                    side_work(s, j, 1)
                    second_pass(s, j, 1)
                    side_work(s, j, 2)
                    late = s.t0 > 0
                    if j == LAG + 1 and late:
                        p_times_c(s, 0)
                    if j >= LAG + late:
                        p_times_c(s, j - LAG)
                    elif j < LAG and s.t0 > 0:
                        p_times_c(s, NT - LAG + j, -1)

            def turn_weights(w, bank, rows, block, i):
                return pe.transpose(bank[:, i * rows:(i + 1) * rows], w[:, block * 128:(block + 1) * 128],
                                    ident[0:rows, 0:rows])

            def turn_x(p):
                pe.wait_ge(xn_done, p + 1)
                bank = scores[:, 0] if p == 0 else pc[:, 0]
                return pe.transpose(bank[:, p * PAIR:(p + 1) * PAIR], xn[:, p, :], ident[0:PAIR, 0:PAIR])

            def product_g(h):
                b = G_BANKS[h // 8 * 2 + h % 2]
                bank = scores[:, 1] if b < 0 else pc[:, b]
                i, part = h % 8 // 2, slice(DH * (h % 2), DH * (h % 2) + DH)
                mm = pe.matmul(bank[:, i * DC:(i + 1) * DC], wqT[part, h // 2, :], wkT[part, h // 2, :],
                               start=True, stop=True)
                if i == 3:
                    mm.then_inc(w_full, 1)

            pro = Prologue()
            def keep_clock_up(products):
                for _ in range(products):
                    pe.matmul(scores[0:PAIR, 1, 0:PAIR], ones[:, :], ones[:, :], start=True, stop=True)

            pe.wait_ge(ones_ready, 1)
            keep_clock_up(WARM_UP)
            pe.wait_ge(const_ready, 1)
            pe.wait_ge(wq_loaded, 16)
            for half in range(2):
                for i in range(4):
                    mm = turn_weights(wq, pc[:, half], D, 4 * half + i, i)
                mm.then_inc(w_full, 1)
            pe.wait_ge(wk_loaded, 16)
            for half in range(2):
                for i in range(4):
                    mm = turn_weights(wk, pc[:, 2 + half], DC, 4 * half + i, i)
                mm.then_inc(w_full, 1)
            turn_x(0).then_inc(xnT_full, 1)
            for k in (0, 1):
                transpose_c(pro, k, k)
            pe.wait_ge(w_act, 2)
            pe.wait_ge(w_dve, 2)
            for h in range(H):
                product_g(h)
                if h == HG - 1:
                    transpose_c(pro, 2, 2)
            pe.wait_ge(xnT_lo_done, 1)
            pe.wait_ge(G_lo_done, 2)
            make_g(pro, 3, 0)
            for p in range(1, NP):
                mm = turn_x(p)
            mm.then_inc(xnT_full, 1)
            pe.wait_ge(wv_loaded, 16)
            for half in range(2):
                for i in range(4):
                    mm = turn_weights(wv, scores[:, half], DC, 4 * half + i, i)
                mm.then_inc(w_full, 1)
                if half == 0:
                    pe.wait_ge(G_lo_done, 4)
                    make_g(pro, 4, 1)
            pe.wait_ge(ident16_ready, 1)
            for k, (what, m, _, _) in enumerate(PREP[5:], 5):
                WORK[what](pro, k, m)
                if what != "max":
                    continue
                if m == 0:
                    pe.wait_ge(xnT_lo_done, 2)
                if m < H:
                    make_g_rest(m)
                if m == H:
                    pe.wait_ge(wo_loaded, 16)
                    pe.wait_ge(w_act, 6)
                for h in M_AT.get(m, []):
                    if h == 4:
                        pe.wait_ge(grest_copied, H)
                    mm = product_m(pc[:, h // 4], h)
                    if h % 4 == 3:
                        mm.then_inc(w_full, 1)
            pe.wait_ge(late_const, 3)
            run_steps(pe, step)
            s = Step(B, TAIL)
            for j in range(NT - LAG, NT):
                p_times_c(s, j, -1)
            for k, (what, m, _, _) in enumerate(TAIL):
                if (what, m) in TAIL_WARM:
                    keep_clock_up(TAIL_WARM[what, m])
                WORK[what](s, k, m)

        @block.scalar
        def _(act):
            act.dma_start(wq[:, :], w_q).then_inc(wq_loaded, 16)
            act.dma_start(wk[:, :], w_k).then_inc(wk_loaded, 16)
            act.dma_start(wo[:, :, :], w_out.rearrange("(b p) n -> p b n", p=128)).then_inc(wo_loaded, 16)
            act.dma_start(bias[:, :], b_out.rearrange("(a n) -> a n", a=1).to_broadcast([PAIR, D]))\
                .then_inc(bias_loaded, 16)

            def ct_hi(s, k, c):
                act.wait_ge(ct_full, s.times(NC, NC + c + 1))
                act.activation(cT_hi[0:DC, (s.t0 + 1) % 2, c * CW:(c + 1) * CW], side[0:DC, k % 2, 0:CW],
                               ACT.Copy).then_inc(ct_hi_done, 1)

            def g_hi_half(s, k, half):
                act.wait_ge(g_full, s.times(2, 2 + half + 1))
                act.activation(g_hi[:, rows_of(s, 1, half * HALF, HALF)],
                               side[0:DC, k % 2, 0:HALF], ACT.Copy, scale=G_DOWN).then_inc(g_hi_done, 1)

            def g_rest_out(head):
                act.wait_ge(grest_full, head + 1)
                source = pc[0:DC, GREST_BANKS[head % 3], 0:REST]
                act.activation(g_rest(g_hi[:, :], head), source.rearrange("c (b q) -> c b q", q=Q), ACT.Copy,
                               scale=G_DOWN)
                act.activation(g32[:, head, :], source, ACT.Copy, scale=G_DOWN).then_inc(grest_copied, 1)

            def m_out(s, k, n):
                act.wait_ge(m_full, n - 1)
                act.activation(M_hi[:, 4 * n:4 * n + 4, :],
                               side[0:DC, k % 2, 0:4 * D].rearrange("p (h c) -> p h c", h=4), ACT.Copy,
                               scale=M_UP).then_inc(M_hi_done, 1)

            def max_row(s, k, m):
                if m == 0:
                    act.wait_ge(mrow_full, s.times(2, 2 + m + 1))
                    act.activation(g_lo[DC:DC + 1, rows_of(s, 1, 0, 512)], side[DC:DC + 1, k % 2, 0:512],
                                   ACT.Copy).then_inc(side_free[k % 2], 1)

            def u_turned(s, k, m):
                act.wait_ge(ut_full, s.times(2, -2 + m + 1))
                for columns, rows in turned_u(s, m):
                    mm = act.activation(columns(uT_hi), rows(side[0:DC, k % 2]), ACT.Copy)
                mm.then_inc(ut_hi_done, 1)

            def rhs_out(s, k, m):
                if m == 1:
                    act.wait_ge(rhs_full, 2)
                    act.activation(rhs_i[:, :], side[:, k % 2, 0:D // 2].bitcast(F16), ACT.Copy)
                    act.activation(rhs_row[:, :], side[0:PAIR, k % 2, D:2 * D], ACT.Copy)\
                        .then_inc(side_free[k % 2], 1)

            WORK = {"ct": ct_hi, "g": g_hi_half, "m": m_out, "mrow": max_row, "ut": u_turned, "rhs": rhs_out}

            def side_work(s, j, place):
                for k, what, m in at(s.schedule, j, place):
                    if what in WORK:
                        WORK[what](s, k, m)

            def exp_half(s, j, half):
                act.wait_ge(scores_full, s.times(2 * NT, 2 * j + half + 1))
                at_least(act, pc_done, s.times(NT, j - NPB + 1))
                act.activation(prob[:, j % NPB, half * HALF:(half + 1) * HALF], scores[0:KP, half, 0:HALF],
                               ACT.Exp).then_inc(exp_done, 1)

            def split_c(s):
                n2 = (s.t0 + 1) % 2
                at_least(act, c_loaded[n2], s.times(8, 24 if not n2 else 16))
                at_least(act, pc_done, s.times(NT))
                act.activation(cn[:, n2, :, 0:DC], c32[:, n2], ACT.Copy).then_inc(c_hi_done, 1)

            def step(s):
                for j in range(NT):
                    side_work(s, j, 0)
                    exp_half(s, j, 0)
                    side_work(s, j, 1)
                    exp_half(s, j, 1)
                    side_work(s, j, 2)
                    if j == 2 and s.t0 < B - 1:
                        split_c(s)

            def copy_weights(full, to, bank, rows):
                act.wait_ge(w_full, full)
                act.activation(to.rearrange("p a c -> p (a c)"), bank[:, 0:4 * rows], ACT.Copy).then_inc(w_act, 1)

            def copy_g(full, heads, bank):
                act.wait_ge(w_full, full)
                act.activation(G_hi[:, heads, :], bank[:, 0:4 * DC].rearrange("p (h c) -> p h c", h=4),
                               ACT.Copy, scale=G_UP).then_inc(G_hi_done, 1)

            def copy_xnT(full, bank, cols):
                act.wait_ge(xnT_full, full)
                act.activation(xnT_hi[:, cols], bank[:, cols], ACT.Copy).then_inc(xnT_hi_done, 1)

            pro = Prologue()
            copy_weights(1, wqT[:, 0:4, :], pc[:, 0], D)
            copy_weights(3, wkT[:, 0:4, :], pc[:, 2], DC)
            copy_xnT(1, scores[:, 0], slice(0, PAIR))
            ct_hi(pro, 0, 0)
            ct_hi(pro, 1, 1)
            for n, bank in enumerate(G_BANKS):
                copy_g(5 + n, EIGHT_HEADS[n], (scores[:, 1] if bank < 0 else pc[:, bank]))
                if n == 1:
                    ct_hi(pro, 2, 2)
            g_hi_half(pro, 3, 0)
            copy_xnT(2, pc[:, 0], slice(PAIR, B * Q))
            act.wait_ge(wvT_zeroed, 1)
            for half in range(2):
                act.wait_ge(w_full, 9 + half)
                for odd in (0, 1):
                    part = slice(DH * odd, DH * odd + DH)
                    act.activation(wvT[part, 8 * half + odd:8 * half + 8:2, :],
                                   scores[part, half, 0:4 * DC].rearrange("p (a c) -> p a c", a=4), ACT.Copy)\
                        .then_inc(w_act, 1)
                if half == 0:
                    g_hi_half(pro, 4, 1)
            for head in range(H):
                g_rest_out(head)
                if head == MROW_AFTER[0] + 1:
                    max_row(pro, use_of(PREP, "mrow", 0), 0)
            split_c(pro)
            for n in range(2):
                act.wait_ge(w_full, 11 + n)
                act.activation(M_hi[:, 4 * n:4 * n + 4, :],
                               pc[0:DC, n, 0:4 * D].rearrange("p (h c) -> p h c", h=4), ACT.Copy,
                               scale=M_UP).then_inc(M_hi_done, 1)
            run_steps(act, step)
            s = Step(B, TAIL)
            for m in range(2):
                u_turned(s, m, m)

        @block.vector
        def _(dve):
            def ct_lo(s, k, c):
                n2 = (s.t0 + 1) % 2
                cols = slice(c * CW, (c + 1) * CW)
                dve.wait_ge(ct_hi_done, s.times(NC, NC + c + 1))
                dve.tensor_tensor(cT_lo[:, n2, cols], side[0:DC, k % 2, 0:CW], cT_hi[0:DC, n2, cols],
                                  ALU.subtract).then_inc(side_free[k % 2], 1)

            def g_lo_half(s, k, half):
                cols = rows_of(s, 1, half * HALF, HALF)
                dve.wait_ge(g_hi_done, s.times(2, 2 + half + 1))
                dve.scalar_tensor_tensor(out=g_lo[0:DC, cols], in0=side[0:DC, k % 2, 0:HALF],
                                         scalar=G_DOWN, in1=g_hi[:, cols], op0=ALU.mult,
                                         op1=ALU.subtract).then_inc(side_free[k % 2], 1)

            def max_row(s, k, m):
                if m == 1:
                    dve.wait_ge(mrow_full, s.times(2, 2 + m + 1))
                    dve.tensor_copy(g_lo[DC:DC + 1, rows_of(s, 1, 512, ROWS - 512)],
                                    side[DC:DC + 1, k % 2, 0:ROWS - 512]).then_inc(side_free[k % 2], 1)

            def chunk_max(s, k, m):
                dve.wait_ge(max_full, s.times(NR * NC, NR * NC + m + 1))
                dve.tensor_reduce(maxes[:, m // NC, m % NC:m % NC + 1], side[:, k % 2, 0:CW], AX.X,
                                  ALU.max).then_inc(side_free[k % 2], 1)
                if m in MROW_AFTER:
                    dve.wait_ge(side_free[k % 2], s.freed(k + 2))
                    at_least(dve, mrow_full, s.times(2, 2))
                    tiles = slice(0, 4) if m == MROW_AFTER[0] else slice(4, NR)
                    dve.tensor_reduce(neg_max[:, tiles], maxes[:, tiles, :], AX.X, ALU.max,
                                      negate=True).then_inc(neg_max_done, 1)

            def take_u(s):
                dve.wait_ge(pc_done, s.times(NT))
                parts = [(slice(0, 4), pc[:, 0:4, 0:CN]), (slice(4, NR), pc[:, 0:NR - 4, CN:2 * CN])]
                for rows, acc in parts:
                    dve.reciprocal(rsum[:, rows], acc[:, :, DC]).then_inc(rsum_done, 1)
                for n, (rows, acc) in enumerate(parts):
                    if s.t0 == B and n == 1:
                        add_parts(dve, s, 0)
                    dve.wait_ge(rsum_done, s.times(2, -2 + n + 1))
                    count = rows.stop - rows.start
                    dve.tensor_tensor(u_part[:, rows, :], acc,
                                      rsum[:, rows].rearrange("p (r a) -> p r a", a=1).to_broadcast([128, count, CN]),
                                      ALU.mult).then_inc(u_part_done, 1)
                if s.t0 == B:
                    add_parts(dve, s, 1)

            def u_low(s, k, m):
                dve.wait_ge(ut_hi_done, s.times(2, -2 + m + 1))
                for columns, rows in turned_u(s, m):
                    mm = dve.tensor_tensor(columns(uT_lo), rows(side[0:DC, k % 2]), columns(uT_hi), ALU.subtract)
                mm.then_inc(side_free[k % 2], 1)

            def m_low(bank, n):
                dve.wait_ge(M_hi_done, n + 1)
                return dve.scalar_tensor_tensor(out=M_lo[:, 4 * n:4 * n + 4, :],
                                                in0=bank[:, 0:4 * D].rearrange("p (h c) -> p h c", h=4),
                                                scalar=M_UP, in1=M_hi[:, 4 * n:4 * n + 4, :], op0=ALU.mult,
                                                op1=ALU.subtract)

            def m_lo_half(s, k, n):
                m_low(side[0:DC, k % 2], n).then_inc(side_free[k % 2], 1)

            def finish_x1(s, k, m):
                dve.wait_ge(out_full, s.pairs(2, m + 1))
                if m == 0:
                    if s.i is None:
                        resid = xb[:, s.pairs(1), :]
                    else:
                        resid = xb[:, bass.ds(s.pairs(1), 1), :].rearrange("p a d -> p (a d)")
                    dve.scalar_tensor_tensor(out=x1_part[:, :], in0=side[0:PAIR, k % 2, 0:D],
                                             scalar=1 / M_UP, in1=resid, op0=ALU.mult, op1=ALU.add)\
                        .then_inc(side_free[k % 2], 1)
                    return
                k0 = [kk for kk, use in enumerate(s.schedule) if use[0] == "out"][0]
                dve.wait_ge(side_free[k0 % 2], s.freed(k0 + 2))
                dve.scalar_tensor_tensor(out=x1[:, :], in0=side[0:PAIR, k % 2, 0:D], scalar=1 / M_UP,
                                         in1=x1_part[:, :], op0=ALU.mult, op1=ALU.add)\
                    .then_inc(side_free[k % 2], 1)
                dve.wait_ge(side_free[k % 2], s.freed(k + 2))
                dve.bn_stats(st2[:, :], x1[:, :]).then_inc(ffn_step, 1)

            def row_moments(s):
                dve.bn_aggr(mv2[:, :], st2[:, :]).then_inc(ffn_step, 1)
                dve.wait_ge(ffn_step, s.pairs(NFFN, 2))
                dve.tensor_scalar(ve2[:, :], mv2[:, 1:2], EPS, None, ALU.add).then_inc(ffn_step, 1)

            def normalise(s):
                dve.wait_ge(rstd2_done, s.pairs(1, 1))
                dve.tensor_scalar(xn2[:, :], x1[:, :], mv2[:, 0:1], rstd2[:, :], ALU.subtract, ALU.mult)\
                    .then_inc(ffn_step, 1)

            def row_max(s):
                dve.wait_ge(ffn_step, s.pairs(NFFN, 4))
                dve.tensor_reduce(row_sc[:, 0:1], xn2[:, :], AX.X, ALU.max, apply_absolute_value=True)\
                    .then_inc(ffn_step, 1)

            def row_scale(s):
                dve.wait_ge(ffn_step, s.pairs(NFFN, 5))
                dve.tensor_scalar(row_sc[:, 1:2], row_sc[:, 0:1], 1e-12, 1.0 / QMAX, ALU.max, ALU.mult)\
                    .then_inc(ffn_step, 1)

            def row_inverse(s):
                dve.wait_ge(ffn_step, s.pairs(NFFN, 6))
                dve.reciprocal(row_sc[:, 2:3], row_sc[:, 1:2]).then_inc(ffn_step, 1)

            def clip_high(s):
                dve.wait_ge(ffn_step, s.pairs(NFFN, 7))
                dve.tensor_scalar(q_a[:, :], xn2[:, :], row_sc[:, 2:3], QMAX, ALU.mult, ALU.min)\
                    .then_inc(ffn_step, 1)

            def clip_low(s):
                dve.wait_ge(ffn_step, s.pairs(NFFN, 8))
                dve.tensor_scalar(q_b[:, :], q_a[:, :], -QMAX, ROUND, ALU.max, ALU.add).then_inc(ffn_step, 1)

            def to_integers(s):
                dve.wait_ge(ffn_step, s.pairs(NFFN, 9))
                dve.tensor_scalar(q_i[:, :], q_b[:, :], ROUND, None, ALU.subtract).then_inc(ffn_step, 1)

            QUANTISE = {(8, 0): normalise, (8, 1): row_max, (8, 2): row_scale, (9, 0): row_inverse,
                        (9, 1): clip_high, (9, 2): clip_low, (10, 0): to_integers}

            def take_qT(s, k, m):
                dve.wait_ge(ft_full, s.pairs(1, 1))
                dve.tensor_copy(q_iT[:, :], side[:, k % 2, 0:PAIR // 2].bitcast(F16))\
                    .then_inc(side_free[k % 2], 1)

            def finish_pair(s, k, m):
                dve.wait_ge(fm_full, s.pairs(1, 1))
                dve.scalar_tensor_tensor(out=y_a[:, :], in0=side[0:PAIR, k % 2, 0:D], scalar=row_sc[:, 1:2],
                                         in1=rhs_row[:, :], op0=ALU.mult, op1=ALU.mult)\
                    .then_inc(side_free[k % 2], 1)
                dve.wait_ge(side_free[k % 2], s.freed(k + 2))
                if s.i is None:
                    y_pair = y[:, s.pairs(1), :]
                else:
                    y_pair = y[:, bass.ds(s.pairs(1), 1), :].rearrange("p a d -> p (a d)")
                dve.tensor_tensor(y_pair, y_a[:, :], x1[:, :], ALU.add).then_inc(y_done, 1)

            def rhs_quantise(s, k, m):
                if m != 0:
                    return
                dve.wait_ge(rhs_full, 1)
                rt = side[:, k % 2, 0:D]
                dve.tensor_reduce(rhs_sc[:, 0:1], rt, AX.X, ALU.max, apply_absolute_value=True)\
                    .then_inc(rhs_step, 1)
                dve.wait_ge(rhs_step, 1)
                dve.tensor_scalar(rhs_sc[:, 1:2], rhs_sc[:, 0:1], 1e-12, 1.0 / QMAX, ALU.max, ALU.mult)\
                    .then_inc(rhs_step, 1)
                dve.wait_ge(rhs_step, 2)
                dve.reciprocal(rhs_sc[:, 2:3], rhs_sc[:, 1:2]).then_inc(rhs_step, 1)
                dve.wait_ge(rhs_step, 3)
                dve.tensor_scalar(rhs_diag[:, :], rt, rhs_sc[:, 2:3], QMAX, ALU.mult, ALU.min)\
                    .then_inc(side_free[k % 2], 1)
                dve.wait_ge(side_free[k % 2], s.freed(k + 2))
                dve.tensor_scalar(rhsT_q[:, :], rhs_diag[:, :], -QMAX, ROUND, ALU.max, ALU.add)\
                    .then_inc(rhs_step, 1)
                dve.wait_ge(rhs_step, 4)
                dve.tensor_scalar(rhsT_i[:, :], rhsT_q[:, :], ROUND, None, ALU.subtract).then_inc(rhs_step, 1)
                dve.tensor_scalar(rhs_diag[:, :], ident[:, :], rhs_sc[:, 1:2], None, ALU.mult)\
                    .then_inc(rhs_step, 1)

            WORK = {"ct": ct_lo, "g": g_lo_half, "ut": u_low, "m": m_lo_half, "max": chunk_max, "mrow": max_row,
                    "out": finish_x1, "ft": take_qT, "fm": finish_pair, "rhs": rhs_quantise}

            def side_work(s, j, place):
                for k, what, m in at(s.schedule, j, place):
                    if what in WORK:
                        WORK[what](s, k, m)

            def prob_low(s, j, half):
                dve.wait_ge(exp_done, s.times(2 * NT, 2 * j + half + 1))
                cols = slice(half * HALF, (half + 1) * HALF)
                dve.tensor_tensor(prob_lo[:, j % NPB, cols], prob[:, j % NPB, cols], prob_hi[:, j % NPB, cols],
                                  ALU.subtract).then_inc(lo_dve, 1)

            def step(s):
                for j in range(NT):
                    if j == 2 and s.t0 > 0:
                        take_u(s)
                    if j in (1, 2) and s.t0 == 0:
                        m_low(pc[0:DC, j - 1], j - 1).then_inc(M_lo_done, 1)
                    pair = s.t0 > 0 and not s.odd
                    side_work(s, j, 0)
                    if pair and (j, 0) in QUANTISE:
                        QUANTISE[j, 0](s)
                    side_work(s, j, 1)
                    if pair and (j, 1) in QUANTISE:
                        QUANTISE[j, 1](s)
                    moments = j == 6 and pair
                    if moments:
                        dve.wait_ge(ffn_step, s.pairs(NFFN, 1))
                    for jh in low_parts(s.t0)[0]:
                        if jh[0] == j:
                            prob_low(s, *jh)
                    if moments:
                        row_moments(s)
                    side_work(s, j, 2)
                    if pair and (j, 2) in QUANTISE:
                        QUANTISE[j, 2](s)

            dve.memset(ones[:, :], 1.0).then_inc(ones_ready, 1)
            dve.memset(minus_half[:, :], -0.5).then_inc(minus_half_ready, 1)
            dve.memset(cn[:, :, :, DC:DC + 1], 1.0).then_inc(late_const, 1)
            dve.memset(cT_hi[DC:DC + 1, 0, :], 1.0).then_inc(late_const, 1)

            def ln_moments(pairs, counted):
                for n, p in enumerate(pairs):
                    dve.bn_stats(st1[:, p, :], x_in[:, p, :]).then_inc(ln_step, 1)
                for n, p in enumerate(pairs):
                    dve.wait_ge(ln_step, counted + n + 1)
                    dve.bn_aggr(mv1[:, p, :], st1[:, p, :]).then_inc(ln_step, 1)
                dve.wait_ge(ln_step, counted + 2 * len(pairs))
                dve.tensor_scalar(ve1[:, pairs[0]:pairs[-1] + 1], mv1[:, pairs[0]:pairs[-1] + 1, 1], EPS, None,
                                  ALU.add).then_inc(ln_step, 1)

            def ln_apply(p):
                dve.tensor_scalar(xn[:, p, :], x_in[:, p, :], mv1[:, p, 0:1], rstd1[:, p:p + 1],
                                  ALU.subtract, ALU.mult).then_inc(xn_done, 1)

            def copy_weights(full, to, bank, rows):
                dve.wait_ge(w_full, full)
                dve.tensor_copy(to.rearrange("p a c -> p (a c)"), bank[:, 0:4 * rows]).then_inc(w_dve, 1)

            def low_g(n):
                heads, bank = EIGHT_HEADS[n], (scores[:, 1] if G_BANKS[n] < 0 else pc[:, G_BANKS[n]])
                dve.wait_ge(G_hi_done, n + 1)
                dve.scalar_tensor_tensor(out=G_lo[:, heads, :],
                                         in0=bank[:, 0:4 * DC].rearrange("p (h c) -> p h c", h=4),
                                         scalar=G_UP, in1=G_hi[:, heads, :], op0=ALU.mult, op1=ALU.subtract)\
                    .then_inc(G_lo_done, 1)

            def low_xnT(hi_done, bank, cols):
                dve.wait_ge(xnT_hi_done, hi_done)
                dve.tensor_tensor(xnT_lo[:, cols], bank[:, cols], xnT_hi[:, cols], ALU.subtract)\
                    .then_inc(xnT_lo_done, 1)

            dve.wait_ge(x_loaded, 16)
            ln_moments([0], 0)
            dve.wait_ge(ln_rstd, 1)
            ln_apply(0)
            dve.wait_ge(x_rest_loaded, 16)
            ln_moments([1, 2, 3], 3)
            copy_weights(2, wqT[:, 4:8, :], pc[:, 1], D)
            copy_weights(4, wkT[:, 4:8, :], pc[:, 3], DC)
            pro = Prologue()
            low_xnT(1, scores[:, 0], slice(0, PAIR))
            dve.wait_ge(ln_rstd, 2)
            for p in range(1, NP):
                ln_apply(p)
            ct_lo(pro, 0, 0)
            ct_lo(pro, 1, 1)
            for n in range(4):
                low_g(n)
                if n == 1:
                    ct_lo(pro, 2, 2)
            g_lo_half(pro, 3, 0)
            low_xnT(2, pc[:, 0], slice(PAIR, B * Q))
            for k, (what, m, _, _) in enumerate(PREP[4:], 4):
                WORK[what](pro, k, m)
            dve.wait_ge(xb_ready, 1)
            run_steps(dve, step)
            s = Step(B, TAIL)
            take_u(s)
            for k, (what, m, _, _) in enumerate(TAIL):
                if what in WORK:
                    WORK[what](s, k, m)
                if (what, m) == ("out", 1):
                    dve.wait_ge(ffn_step, s.pairs(NFFN, 1))
                    row_moments(s)
                    for operation in QUANTISE.values():
                        operation(s)

        @block.gpsimd
        def _(pool):
            def prob_low(s, j, half):
                pool.wait_ge(exp_done, s.times(2 * NT, 2 * j + half + 1))
                cols = slice(half * HALF, (half + 1) * HALF)
                pool.tensor_tensor(prob_lo[:, j % NPB, cols], prob[:, j % NPB, cols], prob_hi[:, j % NPB, cols],
                                   ALU.subtract).then_inc(lo_pool, 1)

            def split_c(s):
                n2 = (s.t0 + 1) % 2
                pool.wait_ge(c_hi_done, s.times(1, 2))
                pool.tensor_tensor(cn[:, n2, :, DC + 1:CN], c32[:, n2], cn[:, n2, :, 0:DC],
                                   ALU.subtract).then_inc(c_lo_done, 1)

            def g_rest_lo(head):
                pool.wait_ge(grest_copied, head + 1)
                pool.tensor_tensor(g_rest(g_lo[0:DC, :], head), g32[:, head, :].rearrange("c (b q) -> c b q", q=Q),
                                   g_rest(g_hi[:, :], head), ALU.subtract).then_inc(grest_lo_done, 1)

            def row_std(s):
                pool.wait_ge(ffn_step, s.pairs(NFFN, 3))
                pool.tensor_tensor(rstd2[:, :], ve2[:, :], minus_half[0:PAIR, 0:1], ALU.pow)\
                    .then_inc(rstd2_done, 1)

            def step(s):
                for j in range(NT):
                    if j == 3 and s.t0 > 0:
                        add_parts(pool, s, 0)
                        add_parts(pool, s, 1)
                    if j == 4 and s.t0 < B - 1:
                        split_c(s)
                    if s.t0 == 0 and 5 <= j < 5 + POOL_REST_LATER:
                        g_rest_lo(H - POOL_REST_LATER + j - 5)
                    if j == 7 and s.t0 > 0 and not s.odd:
                        row_std(s)
                    for jh in low_parts(s.t0)[1]:
                        if jh[0] == j:
                            prob_low(s, *jh)

            pool.memset(ident[:, :], 0.0).then_inc(const_step, 1)
            pool.wait_ge(const_step, 1)
            pool.affine_select(out=ident[:, :], in_=ident[:, :], compare_op=ALU.not_equal, fill=1.0, base=0,
                               pattern=[[-1, 128]], channel_multiplier=1).then_inc(const_ready, 1)
            pool.memset(wvT[:, :, :], 0.0).then_inc(wvT_zeroed, 1)
            pool.wait_ge(minus_half_ready, 1)
            pool.wait_ge(ln_step, 3)
            pool.tensor_tensor(rstd1[:, 0:1], ve1[:, 0:1], minus_half[0:PAIR, 0:1], ALU.pow).then_inc(ln_rstd, 1)
            pool.wait_ge(ln_rstd, 1)
            pool.memset(cT_hi[DC:DC + 1, 1, :], 1.0).then_inc(late_const, 1)
            pool.wait_ge(late_const, 3)
            pool.wait_ge(ln_step, 2 * NP + 2)
            pool.tensor_tensor(rstd1[:, 1:NP], ve1[:, 1:NP], minus_half[0:PAIR, 1:NP], ALU.pow)\
                .then_inc(ln_rstd, 1)
            pool.wait_ge(const_ready, 1)
            pool.tensor_copy(ident16[:, :], ident[:, :]).then_inc(ident16_ready, 1)
            pool.wait_ge(bias_loaded, 16)
            pool.wait_ge(x_rest_loaded, 16)
            pool.tensor_tensor(xb[:, :, :], x_in[:, :, :],
                               bias[:, :].rearrange("p (a d) -> p a d", a=1).to_broadcast([PAIR, NP, D]),
                               ALU.add).then_inc(xb_ready, 1)
            for head in range(H - POOL_REST_LATER):
                g_rest_lo(head)
            split_c(Prologue())
            run_steps(pool, step)
            row_std(Step(B, TAIL))


_INS = ["x", "ctx_768", "L0_xattn_w_q", "L0_xattn_w_k", "L0_xattn_w_v", "L0_xattn_w_out", "L0_xattn_b_out",
        "L0_ffn_rhs"]


def kernel(**inputs):
    import numpy as _np
    import concourse.bacc as _bacc
    from concourse import mybir as _mybir
    from concourse.bass_utils import run_bass_kernel_spmd as _run

    nc = _bacc.Bacc("TRN2", target_bir_lowering=False, num_devices=1)
    arrays, args = {}, []
    for name in _INS:
        a = _np.ascontiguousarray(inputs[name])
        arrays[f"in_{name}"] = a
        args.append(nc.dram_tensor(f"in_{name}", a.shape, _mybir.dt.from_np(a.dtype), kind="ExternalInput").ap())
    args.append(nc.dram_tensor("out_y", (B, Q, D), F32, kind="ExternalOutput").ap())
    build(nc, *args)
    r = _run(nc, [arrays], core_ids=[0])
    return r.results[0]["out_y"]
```
